# Optimizing a Trainium2 kernel written in Bass

```python
import numpy as np
import jax
import jax.numpy as jnp

def _softmax(x, axis=-1):
    return jax.nn.softmax(x, axis=axis)

def _gelu(x):
    return jax.nn.gelu(x, approximate=True)

def _silu(x):
    return jax.nn.silu(x)

def _sigmoid(x):
    return jax.nn.sigmoid(x)

def _layernorm(x, axis=-1, eps=1e-05):
    m = jnp.mean(x, axis=axis, keepdims=True)
    v = jnp.var(x, axis=axis, keepdims=True)
    return (x - m) / jnp.sqrt(v + eps)

def _scatter_add(tgt, idx, src, axis=0):
    return tgt.at[idx].add(src)

def _segment_sum(src, seg, n):
    return jax.ops.segment_sum(src, seg, n)
kernel_name = 'mk_adaln_ffn_d1_seqx_r4_342030'

def setup_inputs(seed: int=0):
    np.random.seed(seed)
    _w = jnp.asarray

    def _rec_inputs():
        import jax
        import jax.numpy as jnp
        _rk = jax.random.key(seed)
        x = -0.000125 + 0.9999 * jax.random.normal(jax.random.fold_in(_rk, 1), (2, 1024, 256), jnp.float32)
        _lenS = 1024 - jax.random.randint(jax.random.fold_in(_rk, 7), (2,), 0, max(1, 1024 // 4) + 1, jnp.int32)
        _lenS2 = 1024 - jax.random.randint(jax.random.fold_in(_rk, 8), (2,), 0, max(1, 1024 // 4) + 1, jnp.int32)
        cond_1024 = -0.00493535 + 1.00056 * jax.random.normal(jax.random.fold_in(_rk, 11), (2, 256), jnp.float32)
        return (x, cond_1024)
    x, cond_1024 = _rec_inputs()

    def _L0_cond_setup():
        import jax, jax.numpy as jnp
        import numpy as np
        import math
        N, T, D, H = (64, 128, 256, 256)
        key = jax.random.key(seed)
        k1, k2, k3, k4 = jax.random.split(key, 4)
        x = jax.random.normal(k1, (N, T, D), dtype=jnp.float32)
        h0 = jax.random.normal(k2, (N, H), dtype=jnp.float32)
        Wx = jax.random.normal(k3, (D, 4 * H), dtype=jnp.float32) / math.sqrt(D)
        Wh = jax.random.normal(k4, (H, 4 * H), dtype=jnp.float32) / math.sqrt(H)
        b = jnp.zeros((4 * H,), dtype=jnp.float32)
        return {'x': x, 'h0': h0, 'Wx': Wx, 'Wh': Wh, 'b': b}
    _L0_cond_all = _L0_cond_setup()
    _L0_cond_in = {k: v for k, v in _L0_cond_all.items() if k in ('Wx', 'Wh', 'b')}
    del _L0_cond_all

    def _L0_ffn_setup():
        import jax, jax.numpy as jnp
        import numpy as np
        DIM = 256
        DEPTH = 6
        HEADS = 16
        DIM_HEAD = 64
        WINDOW = 64
        INNER = HEADS * DIM_HEAD
        DIM_INNER = int(DIM * 4 * 2 / 3)
        QK_SCALE = 8.0

        def shift_tokens(t):
            a, s = jnp.split(t, 2, -1)
            s = jnp.pad(s, ((0, 0), (1, 0), (0, 0)))[:, :-1]
            return jnp.concatenate([a, s], -1)

        def l2norm(t):
            return t / jnp.maximum(jnp.linalg.norm(t, axis=-1, keepdims=True), 1e-12)

        def rotate_half(x):
            x1, x2 = jnp.split(x, 2, -1)
            return jnp.concatenate([-x2, x1], -1)

        def rotary_tables(n):
            half = jnp.arange(0, DIM_HEAD, 2, dtype=jnp.float32)
            inv_freq = 1.0 / 10000.0 ** (half / DIM_HEAD)
            t = jnp.arange(n, dtype=jnp.float32)
            freqs = t[:, None] * inv_freq[None, :]
            freqs = jnp.concatenate([freqs, freqs], -1)
            base_scale = (half + 0.4 * DIM_HEAD) / (1.4 * DIM_HEAD)
            power = (t - n // 2) / (WINDOW // 2)
            scale = base_scale[None, :] ** power[:, None]
            scale = jnp.concatenate([scale, scale], -1)
            return (freqs, scale)

        def local_attention(q, k, v):
            b, h, n, d = q.shape
            w = WINDOW
            nw = n // w
            bq = q.reshape(b, h, nw, w, d)
            bk = k.reshape(b, h, nw, w, d)
            bv = v.reshape(b, h, nw, w, d)

            def look(t):
                p = jnp.pad(t, ((0, 0), (0, 0), (1, 0), (0, 0), (0, 0)))
                return jnp.concatenate([p[:, :, :nw], p[:, :, 1:]], axis=3)
            bk2, bv2 = (look(bk), look(bv))
            seq = jnp.arange(n).reshape(nw, w)
            seq_p = jnp.pad(seq, ((1, 0), (0, 0)), constant_values=-1)
            jt = jnp.concatenate([seq_p[:nw], seq_p[1:]], axis=1)
            it = seq[:, :, None]
            jb = jt[:, None, :]
            mask = (it < jb) | (it > jb + w) | (jb == -1)
            sim = jnp.einsum('bhwie,bhwje->bhwij', bq, bk2) * QK_SCALE
            sim = jnp.where(mask, -jnp.finfo(sim.dtype).max, sim)
            attn = jax.nn.softmax(sim, -1)
            out = jnp.einsum('bhwij,bhwje->bhwie', attn, bv2)
            return out.reshape(b, h, n, d)

        def attn_layer(x, Wqkv, qs, ksc, Wo):
            b, n, _ = x.shape
            qkv = x @ Wqkv
            q, k, v = jnp.split(qkv, 3, -1)
            sh = lambda t: t.reshape(b, n, HEADS, DIM_HEAD).transpose(0, 2, 1, 3)
            q, k, v = (sh(q), sh(k), sh(v))
            q = l2norm(q) * qs
            k = l2norm(k) * ksc
            freqs, scale = rotary_tables(n)
            cos, sin = (jnp.cos(freqs), jnp.sin(freqs))
            q = q * cos * scale + rotate_half(q) * sin * scale
            inv = 1.0 / scale
            k = k * cos * inv + rotate_half(k) * sin * inv
            out = local_attention(q, k, v)
            out = out.transpose(0, 2, 1, 3).reshape(b, n, INNER)
            return out @ Wo

        def ffn_layer(x, g, bln, W1, b1, W2, b2):
            mu = x.mean(-1, keepdims=True)
            var = ((x - mu) ** 2).mean(-1, keepdims=True)
            xn = (x - mu) / jnp.sqrt(var + 1e-05) * g + bln
            hg = xn @ W1 + b1
            a, gate = jnp.split(hg, 2, -1)
            return a * jax.nn.gelu(gate, approximate=False) @ W2 + b2
        key = jax.random.key(seed)
        ks = jax.random.split(key, 8)
        B, N = (2, 512)
        init = lambda k, shape: jax.random.normal(k, shape, jnp.float32) * 0.02
        return {'x': jax.random.normal(ks[0], (B, N, DIM), jnp.float32), 'Wqkv': init(ks[1], (DEPTH, DIM, 3 * INNER)), 'q_scale': jnp.ones((DEPTH, DIM_HEAD), jnp.float32), 'k_scale': jnp.ones((DEPTH, DIM_HEAD), jnp.float32), 'Wo': init(ks[2], (DEPTH, INNER, DIM)), 'ln_g': jnp.ones((DEPTH, DIM), jnp.float32), 'ln_b': jnp.zeros((DEPTH, DIM), jnp.float32), 'W1': init(ks[3], (DEPTH, DIM, 2 * DIM_INNER)), 'b1': jnp.zeros((DEPTH, 2 * DIM_INNER), jnp.float32), 'W2': init(ks[4], (DEPTH, DIM_INNER, DIM)), 'b2': jnp.zeros((DEPTH, DIM), jnp.float32)}
    _L0_ffn_all = _L0_ffn_setup()
    _L0_ffn_in = {k: v for k, v in _L0_ffn_all.items() if k in ('Wqkv', 'q_scale', 'k_scale', 'Wo', 'ln_g', 'ln_b', 'W1', 'b1', 'W2', 'b2')}
    del _L0_ffn_all
    return {'x': x, 'cond_1024': cond_1024, 'L0_cond_Wx': _L0_cond_in['Wx'], 'L0_cond_Wh': _L0_cond_in['Wh'], 'L0_cond_b': _L0_cond_in['b'], 'L0_ffn_Wqkv': _L0_ffn_in['Wqkv'], 'L0_ffn_q_scale': _L0_ffn_in['q_scale'], 'L0_ffn_k_scale': _L0_ffn_in['k_scale'], 'L0_ffn_Wo': _L0_ffn_in['Wo'], 'L0_ffn_ln_g': _L0_ffn_in['ln_g'], 'L0_ffn_ln_b': _L0_ffn_in['ln_b'], 'L0_ffn_W1': _L0_ffn_in['W1'], 'L0_ffn_b1': _L0_ffn_in['b1'], 'L0_ffn_W2': _L0_ffn_in['W2'], 'L0_ffn_b2': _L0_ffn_in['b2']}

def reference(x, cond_1024, L0_cond_Wx, L0_cond_Wh, L0_cond_b, L0_ffn_Wqkv, L0_ffn_q_scale, L0_ffn_k_scale, L0_ffn_Wo, L0_ffn_ln_g, L0_ffn_ln_b, L0_ffn_W1, L0_ffn_b1, L0_ffn_W2, L0_ffn_b2):
    import jax
    import jax.numpy as jnp

    def _L0_cond_ref(x, h0, Wx, Wh, b):
        import jax, jax.numpy as jnp
        import numpy as np
        import math
        N, T, D, H = (64, 128, 256, 256)
        Hdim = h0.shape[1]
        c0 = jnp.zeros_like(h0)
        xW = jnp.einsum('ntd,dk->tnk', x, Wx) + b

        def step(carry, xw_t):
            prev_h, prev_c = carry
            a = xw_t + prev_h @ Wh
            i = jax.nn.sigmoid(a[:, :Hdim])
            f = jax.nn.sigmoid(a[:, Hdim:2 * Hdim])
            o = jax.nn.sigmoid(a[:, 2 * Hdim:3 * Hdim])
            g = jnp.tanh(a[:, 3 * Hdim:])
            next_c = f * prev_c + i * g
            next_h = o * jnp.tanh(next_c)
            return ((next_h, next_c), next_h)
        _, hs = jax.lax.scan(step, (h0, c0), xW)
        return jnp.transpose(hs, (1, 0, 2))

    def _L0_ffn_ref(x, Wqkv, q_scale, k_scale, Wo, ln_g, ln_b, W1, b1, W2, b2):
        import jax, jax.numpy as jnp
        import numpy as np
        DIM = 256
        DEPTH = 6
        HEADS = 16
        DIM_HEAD = 64
        WINDOW = 64
        INNER = HEADS * DIM_HEAD
        DIM_INNER = int(DIM * 4 * 2 / 3)
        QK_SCALE = 8.0

        def shift_tokens(t):
            a, s = jnp.split(t, 2, -1)
            s = jnp.pad(s, ((0, 0), (1, 0), (0, 0)))[:, :-1]
            return jnp.concatenate([a, s], -1)

        def l2norm(t):
            return t / jnp.maximum(jnp.linalg.norm(t, axis=-1, keepdims=True), 1e-12)

        def rotate_half(x):
            x1, x2 = jnp.split(x, 2, -1)
            return jnp.concatenate([-x2, x1], -1)

        def rotary_tables(n):
            half = jnp.arange(0, DIM_HEAD, 2, dtype=jnp.float32)
            inv_freq = 1.0 / 10000.0 ** (half / DIM_HEAD)
            t = jnp.arange(n, dtype=jnp.float32)
            freqs = t[:, None] * inv_freq[None, :]
            freqs = jnp.concatenate([freqs, freqs], -1)
            base_scale = (half + 0.4 * DIM_HEAD) / (1.4 * DIM_HEAD)
            power = (t - n // 2) / (WINDOW // 2)
            scale = base_scale[None, :] ** power[:, None]
            scale = jnp.concatenate([scale, scale], -1)
            return (freqs, scale)

        def local_attention(q, k, v):
            b, h, n, d = q.shape
            w = WINDOW
            nw = n // w
            bq = q.reshape(b, h, nw, w, d)
            bk = k.reshape(b, h, nw, w, d)
            bv = v.reshape(b, h, nw, w, d)

            def look(t):
                p = jnp.pad(t, ((0, 0), (0, 0), (1, 0), (0, 0), (0, 0)))
                return jnp.concatenate([p[:, :, :nw], p[:, :, 1:]], axis=3)
            bk2, bv2 = (look(bk), look(bv))
            seq = jnp.arange(n).reshape(nw, w)
            seq_p = jnp.pad(seq, ((1, 0), (0, 0)), constant_values=-1)
            jt = jnp.concatenate([seq_p[:nw], seq_p[1:]], axis=1)
            it = seq[:, :, None]
            jb = jt[:, None, :]
            mask = (it < jb) | (it > jb + w) | (jb == -1)
            sim = jnp.einsum('bhwie,bhwje->bhwij', bq, bk2) * QK_SCALE
            sim = jnp.where(mask, -jnp.finfo(sim.dtype).max, sim)
            attn = jax.nn.softmax(sim, -1)
            out = jnp.einsum('bhwij,bhwje->bhwie', attn, bv2)
            return out.reshape(b, h, n, d)

        def attn_layer(x, Wqkv, qs, ksc, Wo):
            b, n, _ = x.shape
            qkv = x @ Wqkv
            q, k, v = jnp.split(qkv, 3, -1)
            sh = lambda t: t.reshape(b, n, HEADS, DIM_HEAD).transpose(0, 2, 1, 3)
            q, k, v = (sh(q), sh(k), sh(v))
            q = l2norm(q) * qs
            k = l2norm(k) * ksc
            freqs, scale = rotary_tables(n)
            cos, sin = (jnp.cos(freqs), jnp.sin(freqs))
            q = q * cos * scale + rotate_half(q) * sin * scale
            inv = 1.0 / scale
            k = k * cos * inv + rotate_half(k) * sin * inv
            out = local_attention(q, k, v)
            out = out.transpose(0, 2, 1, 3).reshape(b, n, INNER)
            return out @ Wo

        def ffn_layer(x, g, bln, W1, b1, W2, b2):
            mu = x.mean(-1, keepdims=True)
            var = ((x - mu) ** 2).mean(-1, keepdims=True)
            xn = (x - mu) / jnp.sqrt(var + 1e-05) * g + bln
            hg = xn @ W1 + b1
            a, gate = jnp.split(hg, 2, -1)
            return a * jax.nn.gelu(gate, approximate=False) @ W2 + b2
        for i in range(DEPTH):
            x = attn_layer(shift_tokens(x), Wqkv[i], q_scale[i], k_scale[i], Wo[i]) + x
            x = ffn_layer(shift_tokens(x), ln_g[i], ln_b[i], W1[i], b1[i], W2[i], b2[i]) + x
        return x
    x = x + _L0_ffn_ref(_L0_cond_ref(x, cond_1024, L0_cond_Wx, L0_cond_Wh, L0_cond_b), L0_ffn_Wqkv, L0_ffn_q_scale, L0_ffn_k_scale, L0_ffn_Wo, L0_ffn_ln_g, L0_ffn_ln_b, L0_ffn_W1, L0_ffn_b1, L0_ffn_W2, L0_ffn_b2)
    return x

_drawn_inputs = setup_inputs


def setup_inputs(seed=0):
    import zlib

    import numpy as np

    out = dict(_drawn_inputs(seed))
    spreads = {'L0_cond_b': (0.0, 0.1),
     'L0_ffn_q_scale': (1.0, 0.6),
     'L0_ffn_k_scale': (1.0, 0.6),
     'L0_ffn_ln_g': (1.0, 0.6),
     'L0_ffn_ln_b': (0.0, 0.687),
     'L0_ffn_b1': (0.0, 0.1),
     'L0_ffn_b2': (0.0, 0.1)}
    factors = {'cond_1024': 6.822}
    for name, (base, spread) in spreads.items():
        noise = np.random.default_rng([zlib.crc32(name.encode()), seed]).standard_normal(out[name].shape)
        drawn = base * np.exp(spread * noise) if base else spread * noise
        out[name] = jnp.asarray(drawn.astype(out[name].dtype))
    for name, factor in factors.items():
        out[name] = (out[name] * factor).astype(out[name].dtype)
    return out
```

```python
from contextlib import ExitStack

import concourse.bass as bass
from concourse import mybir

F32 = mybir.dt.float32
BF16 = mybir.dt.bfloat16
ALU = mybir.AluOpType
ACT = mybir.ActivationFunctionType
AX_X = mybir.AxisListType.X

P = 128
BATCH, SEQ, DIM = 2, 1024, 256
KT = DIM // P
DEPTH, HEADS, DHEAD, WINDOW = 6, 16, 64, 64
INNER = HEADS * DHEAD
FF = int(DIM * 4 * 2 / 3)
FCH = (FF + P - 1) // P
FW = [min(P, FF - P * j) for j in range(FCH)]
GATES = 4 * DIM
GM = GATES // P
QK_SCALE = 8.0
LN_EPS = 1e-5
NORM_FLOOR = 1e-24
MASKED = -1.0e30

TILE = 128
GROUP = 512
TPG = GROUP // TILE
GPB = SEQ // GROUP
TPB = SEQ // TILE
XROW = SEQ + 1
STEPS = 4
PARTS = 3
HC = KT * BATCH
XWC = GM * PARTS * BATCH
CHAIN = TPG * (2 * 1 + 2 * 2 + 4 + 4) + (TPG // 2) * 4


class Count:

    def __init__(self, sem, per, start=0):
        self.sem, self.per, self.start, self.n = sem, per, start, 0

    def inc(self, ins):
        self.n += 1
        ins.then_inc(self.sem, 1)
        return self.n

    def done(self):
        assert self.n == self.per, (self.n, self.per)

    def wait(self, eng, it, n):
        eng.wait_ge(self.sem, it * self.per + n)


def build_program(nc, x_cols, h0_cols, Wx, Wh, b_cols, Wqkv, qk_scales, Wo, W1, W2, layer_vecs, rotary, masks, identity, out):
    with ExitStack() as ctx:
        def sb(name, shape, dt=F32, c=ctx):
            return c.enter_context(nc.sbuf_tensor(name, shape, dt))

        def sem(name, c=ctx):
            return c.enter_context(nc.semaphore(name))

        xa = sb("xa", [P, KT, BATCH * XROW])
        xb = sb("xb", [P, KT, BATCH * XROW])
        ident = sb("ident", [P, P])
        ident16 = sb("ident16", [P, P], BF16)
        vecs = sb("vecs", [P, DEPTH, 2 * FCH + 3 * KT])
        lstm_stage(nc, sb, sem, x_cols, h0_cols, Wx, Wh, b_cols, layer_vecs, identity, xa, xb, ident, ident16, vecs)
        layer_stage(nc, sb, sem, x_cols, Wqkv, qk_scales, Wo, W1, W2, rotary, masks, xa, xb, ident, ident16, vecs, out)


def lstm_stage(nc, sb0, sem0, x_cols, h0_cols, Wx, Wh, b_cols, layer_vecs, identity, xa, xb, ident, ident16, vecs):
    with ExitStack() as ctx:
        def sb(name, shape, dt=F32):
            return sb0(name, shape, dt, ctx)

        def sem(name):
            return sem0(name, ctx)

        xw = sb("xw", [P, SEQ, XWC], BF16)
        wh32 = sb("wh32", [P, KT, GATES])
        whp = sb("whp", [P, PARTS, KT, GATES], BF16)
        wx_sb = sb("wx_sb", [P, KT, GATES])
        xT = sb("xT", [P, KT, BATCH * SEQ])
        bias = sb("bias", [P, GM])
        part32 = sb("part32", [P, 2, 512])
        rest32 = sb("rest32", [P, 512])
        state = sb("state", [P, 5 * HC])
        uv = sb("uv", [P, 2 * HC])
        tcell = sb("tcell", [P, HC])
        gsum = sb("gsum", [P, GM * BATCH])
        h32 = sb("h32", [P, HC])
        hrest = sb("hrest", [P, HC])
        hp = sb("hp", [P, KT, PARTS, BATCH], BF16)
        ps = [ctx.enter_context(nc.psum_tensor(f"gates{i}", [P, 512], F32)) for i in range(2)]

        const_in, wx_in, wh_in, h0_in, xt_in = sem("const_in"), sem("wx_in"), sem("wh_in"), sem("h0_in"), sem("xt_in")
        zeroed, prep = sem("zeroed"), sem("prep")
        projected, xw_evac, xw_split, xw_chain = sem("projected"), sem("xw_evac"), sem("xw_split"), sem("xw_chain")
        gates_done, gates_summed, gates_act, uv_done = sem("gates_done"), sem("gates_summed"), sem("gates_act"), sem("uv_done")
        cell_done, cell_tanh, h_hi, h_parts, h_chain = sem("cell_done"), sem("cell_tanh"), sem("h_hi"), sem("h_parts"), sem("h_chain")
        history = sem("history")

        def pairs(ap):
            return ap.rearrange("p (a b) -> p a b", b=BATCH)

        block = ctx.enter_context(nc.Block("lstm"))

        @block.sync
        def _(sp):
            sp.dma_start(ident[:, :], identity).then_inc(const_in, 16)
            sp.dma_start(vecs[:, :, :], layer_vecs).then_inc(const_in, 16)
            sp.dma_start(wx_sb[:, :, :], Wx).then_inc(wx_in, 16)
            sp.dma_start(xT[:, :, :], x_cols).then_inc(xt_in, 16)
            sp.dma_start(wh32[:, :, :], Wh).then_inc(wh_in, 16)
            sp.dma_start(bias[:, :], b_cols).then_inc(h0_in, 16)
            sp.dma_start(h32[:, :], h0_cols).then_inc(h0_in, 16)

        @block.gpsimd
        def _(pool):
            nc.gpsimd.memset(xa[:, :, :], 0.0).then_inc(zeroed, 1)
            nc.gpsimd.memset(xb[:, :, :], 0.0).then_inc(zeroed, 1)
            nc.gpsimd.memset(state[:, :], 0.0).then_inc(zeroed, 1)

        @block.tensor
        def _(pe):
            pe.wait_ge(xt_in, 16)
            pe.wait_ge(wx_in, 16)
            n = 0
            for m in range(GM):
                for c in range(BATCH * SEQ // 512):
                    if n >= 2:
                        pe.wait_ge(xw_evac, n - 1)
                    for k in range(KT):
                        last = nc.tensor.matmul(ps[n % 2][:, :], wx_sb[:, k, m * P:(m + 1) * P], xT[:, k, c * 512:(c + 1) * 512],
                                                start=(k == 0), stop=(k == KT - 1))
                    last.then_inc(projected, 1)
                    n += 1
            pe.wait_ge(xw_split, n)
            pe.wait_ge(prep, 2)
            with pe.Fori(0, SEQ // STEPS) as it:
                for s in range(STEPS):
                    g = ps[s % 2]
                    pe.wait_ge(gates_summed, it * STEPS + s + 1)
                    nc.tensor.matmul(g[:, 0:XWC], ident16[:, :], xw[:, it * STEPS + s, :], start=True, stop=False, skip_group_check=True)
                    pe.wait_ge(h_hi, it * STEPS + s + 1)
                    for m in range(GM):
                        for k in range(KT):
                            nc.tensor.matmul(g[:, m * PARTS * BATCH:m * PARTS * BATCH + BATCH], whp[:, 2, k, m * P:(m + 1) * P],
                                             hp[:, k, 0, :], start=False, stop=False, skip_group_check=True)
                    pe.wait_ge(h_parts, it * STEPS + s + 1)
                    for m in range(GM):
                        for p in (1, 0):
                            for k in range(KT):
                                last = nc.tensor.matmul(g[:, m * PARTS * BATCH:(m + 1) * PARTS * BATCH], whp[:, p, k, m * P:(m + 1) * P],
                                                        hp[:, k, :, :].rearrange("p a b -> p (a b)"), start=False, stop=(m == GM - 1),
                                                        skip_group_check=True)
                    last.then_inc(gates_done, 1)

        @block.scalar
        def _(act):
            act.wait_ge(prep, 1)
            n = 0
            for m in range(GM):
                for c in range(BATCH * SEQ // 512):
                    act.wait_ge(projected, n + 1)
                    if n >= 2:
                        act.wait_ge(xw_split, n - 1)
                    nc.scalar.activation(part32[:, n % 2, :], ps[n % 2][:, :], ACT.Identity, bias=bias[:, m:m + 1],
                                         scale=0.5 if m < 3 * GM // 4 else 1.0).then_inc(xw_evac, 1)
                    n += 1
            with act.Fori(0, SEQ // STEPS) as it:
                for s in range(STEPS):
                    t = it * STEPS + s
                    act.wait_ge(gates_summed, t + 3)
                    nc.scalar.activation(state[:, 0:4 * HC], gsum[:, :], ACT.Tanh).then_inc(gates_act, 1)
                    act.wait_ge(cell_done, t + 1)
                    nc.scalar.activation(tcell[:, :], state[:, 4 * HC:5 * HC], ACT.Tanh, scale=0.5).then_inc(cell_tanh, 1)

        @block.vector
        def _(dve):
            n_chain = [0]

            def link(ins):
                n_chain[0] += 1
                ins.then_inc(xw_chain, 1)
                dve.wait_ge(xw_chain, n_chain[0])

            dve.wait_ge(const_in, 32)
            dve.wait_ge(h0_in, 32)
            link(nc.vector.tensor_copy(ident16[:, :], ident[:, :]))
            nc.vector.tensor_scalar(bias[:, 0:3 * GM // 4], bias[:, 0:3 * GM // 4], 0.5, None, ALU.mult).then_inc(prep, 1)
            dve.wait_ge(wh_in, 16)
            for k in range(KT):
                for c in range(GATES // 512):
                    cols = slice(c * 512, (c + 1) * 512)
                    w = wh32[:, k, cols]
                    sig = min(512, 3 * DIM - c * 512)
                    link(nc.vector.tensor_scalar(w[:, 0:sig], w[:, 0:sig], 0.25, None, ALU.mult))
                    if sig < 512:
                        link(nc.vector.tensor_scalar(w[:, sig:512], w[:, sig:512], 0.5, None, ALU.mult))
                    link(nc.vector.tensor_copy(whp[:, 0, k, cols], w))
                    link(nc.vector.tensor_tensor(w, w, whp[:, 0, k, cols], ALU.subtract))
                    link(nc.vector.tensor_copy(whp[:, 1, k, cols], w))
                    link(nc.vector.tensor_tensor(whp[:, 2, k, cols], w, whp[:, 1, k, cols], ALU.subtract))
            link(nc.vector.tensor_scalar(h32[:, :], h32[:, :], 2.0, None, ALU.mult))
            link(nc.vector.tensor_copy(hp[:, :, 0, :], pairs(h32[:, :])))
            link(nc.vector.tensor_tensor(pairs(hrest[:, :]), pairs(h32[:, :]), hp[:, :, 0, :], ALU.subtract))
            link(nc.vector.tensor_copy(hp[:, :, 1, :], pairs(hrest[:, :])))
            link(nc.vector.tensor_tensor(hp[:, :, 2, :], pairs(hrest[:, :]), hp[:, :, 1, :], ALU.subtract))
            n = 0
            for m in range(GM):
                for c in range(BATCH * SEQ // 512):
                    bb, t0 = c // (SEQ // 512), (c % (SEQ // 512)) * 512
                    dve.wait_ge(xw_evac, n + 1)
                    src = part32[:, n % 2, :]
                    at = [xw[:, t0:t0 + 512, (m * PARTS + q) * BATCH + bb] for q in range(PARTS)]
                    link(nc.vector.tensor_copy(at[0], src))
                    link(nc.vector.tensor_tensor(rest32[:, :], src, at[0], ALU.subtract))
                    link(nc.vector.tensor_copy(at[1], rest32[:, :]))
                    ins = nc.vector.tensor_tensor(at[2], rest32[:, :], at[1], ALU.subtract)
                    ins.then_inc(xw_split, 1)
                    dve.wait_ge(xw_split, n + 1)
                    n += 1
            dve.wait_ge(zeroed, 3)
            dve.sem_inc(gates_summed, 2)
            dve.sem_inc(h_hi, 1)
            dve.sem_inc(h_parts, 1)
            dve.sem_inc(prep, 1)
            with dve.Fori(0, SEQ // STEPS) as it:
                for s in range(STEPS):
                    t = it * STEPS + s
                    dve.wait_ge(gates_done, t + 1)
                    nc.vector.tensor_reduce(gsum[:, :].rearrange("p (m b) -> p m b", b=BATCH),
                                            ps[s % 2][:, 0:XWC].rearrange("p (m q b) -> p m b q", q=PARTS, b=BATCH),
                                            AX_X, ALU.add).then_inc(gates_summed, 1)
                    dve.wait_ge(gates_act, t + 1)
                    nc.vector.scalar_tensor_tensor(uv[:, :], state[:, 0:2 * HC], 1.0, state[:, 3 * HC:5 * HC], ALU.add, ALU.mult).then_inc(uv_done, 1)
                    dve.wait_ge(uv_done, t + 1)
                    nc.vector.scalar_tensor_tensor(state[:, 4 * HC:5 * HC], uv[:, HC:2 * HC], 0.5, uv[:, 0:HC], ALU.mult, ALU.add).then_inc(cell_done, 1)
                    dve.wait_ge(cell_tanh, t + 1)
                    og, tcs = pairs(state[:, 2 * HC:3 * HC]), pairs(tcell[:, :])
                    nc.vector.scalar_tensor_tensor(hp[:, :, 0, :], og, 1.0, tcs, ALU.add, ALU.mult).then_inc(h_hi, 1)
                    nc.vector.scalar_tensor_tensor(h32[:, :], state[:, 2 * HC:3 * HC], 1.0, tcell[:, :], ALU.add, ALU.mult).then_inc(h_chain, 1)
                    dve.wait_ge(h_hi, t + 2)
                    dve.wait_ge(h_chain, 2 * t + 1)
                    nc.vector.tensor_tensor(hp[:, :, 1, :], pairs(h32[:, :]), hp[:, :, 0, :], ALU.subtract).then_inc(h_chain, 1)
                    nc.vector.tensor_tensor(pairs(hrest[:, :]), pairs(h32[:, :]), hp[:, :, 0, :], ALU.subtract).then_inc(history, 1)
                    dve.wait_ge(h_chain, 2 * t + 2)
                    dve.wait_ge(history, 2 * t + 1)
                    nc.vector.tensor_tensor(hp[:, :, 2, :], pairs(hrest[:, :]), hp[:, :, 1, :], ALU.subtract).then_inc(h_parts, 1)
                    for k in range(KT):
                        last = nc.vector.tensor_scalar(xa[:, k, :].rearrange("p (b c) -> p b c", c=XROW)[:, :, bass.ds(t + k, 1)].rearrange("p b c -> p (b c)"),
                                                       h32[:, k * BATCH:(k + 1) * BATCH], 0.5, None, ALU.mult)
                    last.then_inc(history, 1)
            dve.wait_ge(history, 2 * SEQ)


def layer_stage(nc, sb0, sem0, x_cols, Wqkv, qk_scales, Wo, W1, W2, rotary, masks, xa, xb, ident, ident16, vecs, out):
    with ExitStack() as ctx:
        def sb(name, shape, dt=F32):
            return sb0(name, shape, dt, ctx)

        def sem(name):
            return sem0(name, ctx)

        HALF = DHEAD // 2
        HG = 4
        wqkv = sb("wqkv", [P, KT, 3 * INNER])
        wo = sb("wo", [P, INNER // P, DIM])
        w1 = sb("w1", [P, KT, 2 * FF])
        w2 = sb("w2", [P, FCH, DIM])
        rot = sb("rot", [P, TPB, 4, DHEAD])
        rotl = sb("rotl", [P, TPB, 4, DHEAD])
        scales = sb("scales", [P, 4 * DHEAD])
        mask = sb("mask", [P, 2, TILE], BF16)
        vec = sb("vec", [P, 2 * FCH + 3 * KT])
        edge = sb("edge", [P, GPB + 1])
        xs = sb("xs", [P, 2, KT, TILE])
        raw = sb("raw", [P, 4, 512])
        sq = sb("sq", [P, 4, 512])
        qk = sb("qk", [P, 4, 512])
        turn = sb("turn", [P, 2, 512])
        ss = sb("ss", [P, 4, 8])
        qn = sb("qn", [P, 2, HEADS])
        kn = sb("kn", [P, HEADS])
        power = sb("power", [P, 8])
        va = sb("va", [P, 2, INNER])
        vb = sb("vb", [P, 2, INNER])
        qT = sb("qT", [P, HEADS // 2, TILE])
        kT = sb("kT", [P, 2, HEADS // 2, 3 * WINDOW])
        mx = sb("mx", [P, HEADS])
        nb = sb("nb", [P, HEADS])
        den = sb("den", [P, HEADS])
        rden = sb("rden", [P, HEADS])
        u = sb("u", [P, FCH, GROUP])
        pr, pT = u[:, 0:2, :], u[:, 2:4, :]
        oT = sb("oT", [P, INNER // P, GROUP])
        xs2 = sb("xs2", [P, KT, GROUP])
        stats = sb("stats", [P, TPG, 6])
        mv = sb("mv", [P, TPG, 2])
        rstd = sb("rstd", [P, TPG])
        xn = sb("xn", [P, TPG, DIM])
        xnT = sb("xnT", [P, KT, GROUP])
        gel = sb("gel", [P, 2, GROUP])

        def pb(name):
            return ctx.enter_context(nc.psum_tensor(name, [P, 512], F32))

        mm = [pb("mm0"), pb("mm1")]
        dd = [pb("dd0"), pb("dd1")]
        tt = [pb("tt0"), pb("tt1")]
        st = [pb("st0"), pb("st1")]

        wqkv_in, wo_in, w1_in, w2_in, sc_in, cst_in = (sem(n) for n in ("wqkv_in", "wo_in", "w1_in", "w2_in", "scales_in", "cst_in"))
        final_in, final_summed, final_out = sem("final_in"), sem("final_summed"), sem("final_out")
        cleared = sem("cleared")
        NPL = BATCH * GPB

        pe_mm = Count(sem("pe_mm"), 6 * TPG + FCH)
        act_mm = Count(sem("act_mm"), 6 * TPG + FCH, 2)
        pe_dd = Count(sem("pe_dd"), 2 * TPG + KT + TPG // 2 + FCH + KT)
        dve_dd = Count(sem("dve_dd"), 2 * TPG + KT + TPG // 2 + FCH + KT, 2)
        pe_tt = Count(sem("pe_tt"), 8 * TPG + KT)
        act_tt = Count(sem("act_tt"), 8 * TPG + KT, 2)
        pe_st = Count(sem("pe_st"), HG * TPG)
        act_st = Count(sem("act_st"), HG * TPG, 2)
        xs_in = Count(sem("xs_in"), TPG)
        xs_used = Count(sem("xs_used"), TPG, 2)
        xs2_in = Count(sem("xs2_in"), 1)
        ss_in = Count(sem("ss_in"), 4 * TPG)
        norm_in = Count(sem("norm_in"), 4 * TPG)
        var_in = Count(sem("var_in"), TPG // 2)
        rstd_in = Count(sem("rstd_in"), TPG // 2)
        turn_in = Count(sem("turn_in"), 4 * TPG)
        qk_in = Count(sem("qk_in"), 4 * TPG, 4)
        nb_in = Count(sem("nb_in"), HG * TPG)
        pr_in = Count(sem("pr_in"), HG * TPG)
        v_in = Count(sem("v_in"), 2 * TPG)
        chain = Count(sem("dve_chain"), CHAIN)
        edge_in = Count(sem("edge_in"), 1)
        attn_out = Count(sem("attn_out"), KT)
        ffn_out = Count(sem("ffn_out"), KT, KT * NPL)
        pool_passed, dve_passed = sem("pool_passed"), sem("dve_passed")
        rotl_in, vec_in = sem("rotl_in"), sem("vec_in")

        def mm_q(i, c): return 6 * i + c + 1
        def mm_gate(j): return 6 * TPG + j + 1
        def dd_o(i, half): return 2 * i + half + 1
        def dd_wo(m): return 2 * TPG + m + 1
        def dd_ft(pq): return 2 * TPG + KT + pq + 1
        def dd_a(j): return 2 * TPG + KT + TPG // 2 + j + 1
        def dd_w2(m): return 2 * TPG + KT + TPG // 2 + FCH + m + 1
        def tt_qk(i, c): return 8 * i + c + 1
        def tt_p(i, g): return 8 * i + 4 + g + 1
        def tt_ln(k): return 8 * TPG + k + 1

        def bank(banks, use): return banks[(use - 1) % 2]

        def freed(eng, sem_, it, use):
            sem_.wait(eng, it, use)

        def done(eng, sem_, it, use):
            sem_.wait(eng, it, use + sem_.start)

        def head_of(g, n):
            return 8 * (g // 2) + g % 2 + 2 * n

        def vcol(j, n=1): return vec[:, j:j + n]
        B1A, B1G, LNG, LNB, B2 = 0, FCH, 2 * FCH, 2 * FCH + KT, 2 * FCH + 2 * KT

        def heads(ap, n=8): return ap.rearrange("p (h d) -> p h d", h=n)

        def loop(eng, body, layer_start=None):
            with eng.Fori(0, DEPTH) as l:
                if layer_start:
                    layer_start(l)
                with eng.Fori(0, BATCH) as bt:
                    with eng.Fori(0, GPB) as h:
                        body(l, bt, h, (l * BATCH + bt) * GPB + h)

        block = ctx.enter_context(nc.Block("layers"))

        @block.sync
        def _(sp):
            sp.dma_start(mask[:, :, :], masks.rearrange("a p n -> p a n")).then_inc(cst_in, 16)
            sp.dma_start(rot[:, :, :, :], rotary.rearrange("(t p) a d -> p t a d", p=P)).then_inc(cst_in, 16)

            def load_scales(l):
                sp.dma_start(scales[:, :], qk_scales[bass.ds(l, 1), :].partition_broadcast(P).rearrange("p a n -> p (a n)")).then_inc(sc_in, 16)

            def load_wqkv(l):
                sp.dma_start(wqkv[:, :, :].rearrange("p k n -> p (k n)"), Wqkv[bass.ds(l, 1), :, :].rearrange("a p n -> (a p) n")).then_inc(wqkv_in, 16)

            def load_wo(l):
                sp.dma_start(wo[:, :, :].rearrange("p k n -> p (k n)"), Wo[bass.ds(l, 1), :, :].rearrange("a p n -> (a p) n")).then_inc(wo_in, 16)

            def load_w1(l):
                sp.dma_start(w1[:, :, :].rearrange("p k n -> p (k n)"), W1[bass.ds(l, 1), :, :].rearrange("a p n -> (a p) n")).then_inc(w1_in, 16)

            def load_w2(l):
                sp.dma_start(w2[:, :, :].rearrange("p k n -> p (k n)"), W2[bass.ds(l, 1), :, :].rearrange("a p n -> (a p) n")).then_inc(w2_in, 16)

            load_scales(0)
            load_wqkv(0)
            load_wo(0)
            load_w1(0)
            load_w2(0)
            with sp.Fori(0, DEPTH - 1) as l:
                last = l * NPL + (NPL - 1)
                sp.wait_ge(rotl_in, l + 1)
                load_scales(l + 1)
                pe_mm.wait(sp, last, mm_q(TPG - 1, 5))
                load_wqkv(l + 1)
                pe_dd.wait(sp, last, dd_wo(KT - 1))
                load_wo(l + 1)
                pe_dd.wait(sp, last, dd_a(FCH - 1))
                load_w1(l + 1)
                pe_dd.wait(sp, last, dd_w2(KT - 1))
                load_w2(l + 1)
            ffn_out.wait(sp, DEPTH * NPL - 1, KT + ffn_out.start)
            sp.dma_start(oT[:, :, :].rearrange("p k n -> p (k n)"), x_cols.rearrange("p k n -> p (k n)")).then_inc(final_in, 16)
            for n in range(KT * BATCH):
                sp.wait_ge(final_summed, n + 1)
                k, bt = n // BATCH, n % BATCH
                sp.dma_start(out[:, k, bt * SEQ:(bt + 1) * SEQ], xa[:, k, bt * XROW + k:bt * XROW + k + SEQ]).then_inc(final_out, 16)
            sp.wait_ge(final_out, 16 * KT * BATCH)

        @block.gpsimd
        def _(pool):
            nc.gpsimd.memset(edge[:, :], 0.0).then_inc(cleared, 1)
            nc.gpsimd.memset(kT[:, :, :, :], 0.0).then_inc(cleared, 1)
            nc.gpsimd.memset(va[:, :, :], 0.0).then_inc(cleared, 1)
            nc.gpsimd.memset(power[:, :], -0.5).then_inc(cleared, 1)
            pool.wait_ge(cleared, 4)
            pool.wait_ge(cst_in, 32)

            def layer_start(l):
                pool.wait_ge(sc_in, (l + 1) * 16)
                done(pool, qk_in, l * NPL, 0)
                nc.gpsimd.tensor_tensor(rotl[:, :, :, :].rearrange("p t a d -> p t (a d)"), rot[:, :, :, :].rearrange("p t a d -> p t (a d)"),
                                        scales[:, :].rearrange("p (o n) -> p o n", o=1).broadcast_to([P, TPB, 4 * DHEAD]),
                                        ALU.mult).then_inc(rotl_in, 1)
                pool.wait_ge(rotl_in, l + 1)
                done(pool, ffn_out, l * NPL, 0)
                nc.gpsimd.tensor_copy(vec[:, :], vecs[:, bass.ds(l, 1), :].rearrange("p a n -> p (a n)")).then_inc(vec_in, 1)

            def body(l, bt, h, it):
                base = bt * XROW + h * GROUP

                def load_xs(i):
                    if i == 0:
                        ffn_out.wait(pool, it, KT)
                    freed(pool, xs_used, it, i + 1)
                    if i == 0:
                        nc.gpsimd.tensor_copy(xs[:, 0, 0, :], xa[:, 0, bass.ds(base, TILE)])
                        nc.gpsimd.tensor_copy(xs[:, 0, 1, 1:TILE], xa[:, 1, bass.ds(base + 1, TILE - 1)])
                        edge_in.inc(nc.gpsimd.tensor_copy(edge[:, bass.ds(h + 1, 1)], xa[:, 1, bass.ds(base + GROUP, 1)]))
                        xs_in.inc(nc.gpsimd.tensor_copy(xs[:, 0, 1, 0:1], edge[:, bass.ds(h, 1)]))
                    else:
                        xs_in.inc(nc.gpsimd.tensor_copy(xs[:, i % 2, :, :], xa[:, :, bass.ds(base + i * TILE, TILE)]))

                def turns(i):
                    for c in range(4):
                        use = 4 * i + c + 1
                        done(pool, act_mm, it, mm_q(i, c))
                        qk_in.wait(pool, it, use + 2)
                        pool.sem_inc(pool_passed, 1)
                        src = raw[:, c, :].rearrange("p (h a d) -> p h a d", a=2, d=HALF)
                        dst = turn[:, c % 2, :].rearrange("p (h a d) -> p h a d", a=2, d=HALF)
                        tab = rotl[:, bass.ds(h * TPG + i, 1), 2 * (c % 2) + 1, :].rearrange("p o (a d) -> p o a d", a=2)
                        for a in range(2):
                            ins = nc.gpsimd.tensor_tensor(dst[:, :, a, :], src[:, :, 1 - a, :],
                                                          tab[:, :, a, :].broadcast_to([P, 8, HALF]), ALU.mult)
                        turn_in.inc(ins)
                        ss_in.wait(pool, it, use)
                        hs = slice(8 * (c // 2), 8 * (c // 2) + 8)
                        norm_in.inc(nc.gpsimd.tensor_tensor(qn[:, i % 2, hs] if c % 2 == 0 else kn[:, hs], ss[:, c, :], power[:, 0:8], ALU.pow))

                load_xs(0)
                turns(0)
                for i in range(1, TPG):
                    load_xs(i)
                    turns(i)
                attn_out.wait(pool, it, KT)
                xs2_in.inc(nc.gpsimd.tensor_copy(xs2[:, :, :], xb[:, :, bass.ds(base, GROUP)]))
                for pq in range(TPG // 2):
                    var_in.wait(pool, it, pq + 1)
                    ts = slice(2 * pq, 2 * pq + 2)
                    rstd_in.inc(nc.gpsimd.tensor_tensor(rstd[:, ts], mv[:, ts, 1], power[:, 0:2], ALU.pow))

            loop(pool, body, layer_start)

        @block.tensor
        def _(pe):
            pe.wait_ge(cleared, 4)
            pe.wait_ge(cst_in, 32)

            def body(l, bt, h, it):
                def project(i, chunks):
                    if chunks[0] == 0:
                        xs_in.wait(pe, it, i + 1)
                    for c in chunks:
                        col = (c // 2) * 512 + (c % 2) * INNER if c < 4 else 2 * INNER + (c - 4) * 512
                        use = mm_q(i, c)
                        freed(pe, act_mm, it, use)
                        for k in range(KT):
                            last = nc.tensor.matmul(bank(mm, use)[:, :], xs[:, i % 2, k, :], wqkv[:, k, col:col + 512],
                                                    start=(k == 0), stop=(k == KT - 1))
                        pe_mm.inc(last)

                def turn_qk(i):
                    for c in range(4):
                        use = tt_qk(i, c)
                        qk_in.wait(pe, it, 4 * i + c + 1 + qk_in.start)
                        freed(pe, act_tt, it, use)
                        for j in range(4):
                            last = nc.tensor.transpose(bank(tt, use)[:, j * TILE:(j + 1) * TILE], qk[:, c, j * P:(j + 1) * P], ident[:, :])
                        pe_tt.inc(last)

                def scores(i, g):
                    use = HG * i + g + 1
                    freed(pe, act_st, it, use)
                    done(pe, act_tt, it, tt_qk(i, 1 if g < 2 else 3))
                    which = h if i == 0 else 1
                    bk = bank(st, use)
                    nc.tensor.matmul(bk[:, :].rearrange("p (g n) -> p g n", g=HG), ident16[:, :],
                                     mask[:, bass.ds(which, 1), :].broadcast_to([P, HG, TILE]), start=True, stop=False, skip_group_check=True)
                    for w in range(2):
                        for n in range(HG):
                            pair, lo = 4 * (g // 2) + n, DHEAD * (g % 2)
                            keys = kT[lo:lo + DHEAD, i % 2, pair, :].rearrange("p (c x) -> p c x", x=WINDOW)
                            keys = keys[:, 0:3:2, :] if w == 0 else keys[:, 0:2, :]
                            last = nc.tensor.matmul(bk[w * WINDOW:(w + 1) * WINDOW, n * TILE:(n + 1) * TILE].rearrange("p (c x) -> p c x", x=WINDOW),
                                                    qT[lo:lo + DHEAD, pair, w * WINDOW:(w + 1) * WINDOW], keys,
                                                    start=False, stop=(n == HG - 1), skip_group_check=True)
                    pe_st.inc(last)

                def turn_p(i, g):
                    use = tt_p(i, g)
                    pr_in.wait(pe, it, HG * i + g + 1)
                    freed(pe, act_tt, it, use)
                    for n in range(HG):
                        last = nc.tensor.transpose(bank(tt, use)[:, n * TILE:(n + 1) * TILE], pr[:, g % 2, n * TILE:(n + 1) * TILE], ident[:, :])
                    pe_tt.inc(last)

                def values(i, g):
                    use = dd_o(i, g // 2)
                    if g % 2 == 0:
                        freed(pe, dve_dd, it, use)
                    v_in.wait(pe, it, 2 * i + g // 2 + 1)
                    done(pe, act_tt, it, tt_p(i, g))
                    bk = bank(dd, use)
                    for n in range(HG):
                        head = head_of(g, n)
                        lo, col = DHEAD * (g % 2), n * TILE
                        for w, v in ((0, va), (1, vb)):
                            last = nc.tensor.matmul(bk[lo:lo + DHEAD, col + w * WINDOW:col + (w + 1) * WINDOW],
                                                    v[:, i % 2, head * DHEAD:(head + 1) * DHEAD],
                                                    pT[:, g % 2, n * TILE + w * WINDOW:n * TILE + (w + 1) * WINDOW],
                                                    start=True, stop=True, skip_group_check=True)
                    if g % 2 == 1:
                        pe_dd.inc(last)

                pe.wait_ge(wqkv_in, (l + 1) * 16)
                project(0, range(6))
                for i in range(TPG):
                    turn_qk(i)
                    scores(i, 0)
                    scores(i, 1)
                    if i + 1 < TPG:
                        project(i + 1, (0, 1))
                    turn_p(i, 0)
                    values(i, 0)
                    scores(i, 2)
                    if i + 1 < TPG:
                        project(i + 1, (2, 3))
                    turn_p(i, 1)
                    values(i, 1)
                    scores(i, 3)
                    if i + 1 < TPG:
                        project(i + 1, (4, 5))
                    turn_p(i, 2)
                    values(i, 2)
                    turn_p(i, 3)
                    values(i, 3)
                pe.wait_ge(wo_in, (l + 1) * 16)
                done(pe, dve_dd, it, dd_o(TPG - 1, 1))
                for m in range(KT):
                    use = dd_wo(m)
                    freed(pe, dve_dd, it, use)
                    for k in range(INNER // P):
                        last = nc.tensor.matmul(bank(dd, use)[:, :], wo[:, k, m * P:(m + 1) * P], oT[:, k, :],
                                                start=(k == 0), stop=(k == INNER // P - 1))
                    pe_dd.inc(last)
                xs2_in.wait(pe, it, 1)
                for pq in range(TPG // 2):
                    use = dd_ft(pq)
                    freed(pe, dve_dd, it, use)
                    for i in range(2):
                        for k in range(KT):
                            last = nc.tensor.transpose(bank(dd, use)[:, (i * KT + k) * P:(i * KT + k + 1) * P],
                                                       xs2[:, k, (2 * pq + i) * TILE:(2 * pq + i + 1) * TILE], ident[:, :])
                    pe_dd.inc(last)
                done(pe, dve_dd, it, dd_ft(TPG // 2 - 1))
                for k in range(KT):
                    use = tt_ln(k)
                    freed(pe, act_tt, it, use)
                    for i in range(TPG):
                        last = nc.tensor.transpose(bank(tt, use)[:, i * TILE:(i + 1) * TILE], xn[:, i, k * P:(k + 1) * P], ident[:, :])
                    pe_tt.inc(last)
                pe.wait_ge(w1_in, (l + 1) * 16)
                done(pe, act_tt, it, tt_ln(KT - 1))
                for j in range(FCH):
                    for use, bk, src, cnt, col in ((mm_gate(j), mm, act_mm, pe_mm, FF), (dd_a(j), dd, dve_dd, pe_dd, 0)):
                        freed(pe, src, it, use)
                        for k in range(KT):
                            last = nc.tensor.matmul(bank(bk, use)[0:FW[j], :], w1[:, k, col + j * P:col + j * P + FW[j]], xnT[:, k, :],
                                                    start=(k == 0), stop=(k == KT - 1))
                        cnt.inc(last)
                pe.wait_ge(w2_in, (l + 1) * 16)
                for m in range(KT):
                    use = dd_w2(m)
                    freed(pe, dve_dd, it, use)
                    for k in range(FCH):
                        if m == 0:
                            done(pe, dve_dd, it, dd_a(k))
                        last = nc.tensor.matmul(bank(dd, use)[:, :], w2[0:FW[k], k, m * P:(m + 1) * P], u[0:FW[k], k, :],
                                                start=(k == 0), stop=(k == FCH - 1))
                    pe_dd.inc(last)

            loop(pe, body)
            for c in (pe_mm, pe_dd, pe_tt, pe_st):
                c.done()

        @block.scalar
        def _(act):
            act.sem_inc(act_mm.sem, act_mm.start)
            act.sem_inc(act_tt.sem, act_tt.start)
            act.sem_inc(act_st.sem, act_st.start)
            act.sem_inc(xs_used.sem, xs_used.start)
            act.wait_ge(cleared, 4)

            def copy(dst, src, **kw):
                return nc.scalar.activation(dst, src, ACT.Identity, **kw)

            def body(l, bt, h, it):
                def take_qk(i, chunks):
                    for c in chunks:
                        use, n = mm_q(i, c), 4 * i + c + 1
                        pe_mm.wait(act, it, use)
                        qk_in.wait(act, it, n)
                        src = bank(mm, use)
                        nc.scalar.activation(sq[:, c, :], src[:, :], ACT.Square)
                        act_mm.inc(copy(raw[:, c, :], src[:, :]))

                def take_v(i):
                    par = i % 2
                    for c in (4, 5):
                        use = mm_q(i, c)
                        pe_mm.wait(act, it, use)
                        src = bank(mm, use)
                        cols = slice((c - 4) * 512, (c - 3) * 512)
                        xin = copy(va[0:WINDOW, par, cols], src[0:WINDOW, :])
                        if c == 5:
                            xs_used.inc(xin)
                        v_in.inc(copy(vb[:, par, cols], src[:, :]))
                        act_mm.inc(copy(va[WINDOW:P, 1 - par, cols], src[WINDOW:P, :]))

                def take_turned(i):
                    for c in range(4):
                        use = tt_qk(i, c)
                        pe_tt.wait(act, it, use)
                        src = bank(tt, use)[:, :].rearrange("p (j t) -> p j t", j=4)
                        pairs_ = slice((c // 2) * 4, (c // 2) * 4 + 4)
                        if c % 2 == 0:
                            act_tt.inc(copy(qT[:, pairs_, :], src))
                        else:
                            copy(kT[:, 1 - i % 2, pairs_, 2 * WINDOW:3 * WINDOW], src[:, :, WINDOW:2 * WINDOW])
                            act_tt.inc(copy(kT[:, i % 2, pairs_, 0:2 * WINDOW], src))

                def exps(i, g):
                    use = HG * i + g + 1
                    nb_in.wait(act, it, use)
                    src = bank(st, use)
                    for n in range(HG):
                        head, at = head_of(g, n), HG * g + n
                        ins = nc.scalar.activation(pr[:, g % 2, n * TILE:(n + 1) * TILE], src[:, n * TILE:(n + 1) * TILE], ACT.Exp,
                                                   bias=nb[:, at:at + 1], scale=qn[:, i % 2, head:head + 1],
                                                   accum_out=den[:, at:at + 1])
                    act_st.inc(ins)

                def take_p(i, g):
                    use = tt_p(i, g)
                    pe_tt.wait(act, it, use)
                    act_tt.inc(copy(pT[:, g % 2, :], bank(tt, use)[:, :]))

                take_qk(0, range(4))
                take_v(0)
                for i in range(TPG):
                    take_turned(i)
                    exps(i, 0)
                    exps(i, 1)
                    if i + 1 < TPG:
                        take_qk(i + 1, (0, 1))
                    take_p(i, 0)
                    exps(i, 2)
                    if i + 1 < TPG:
                        take_qk(i + 1, (2, 3))
                    take_p(i, 1)
                    exps(i, 3)
                    take_p(i, 2)
                    take_p(i, 3)
                    if i + 1 < TPG:
                        pe_dd.wait(act, it, dd_o(i, 1))
                        take_v(i + 1)
                act.wait_ge(vec_in, l + 1)
                for k in range(KT):
                    use = tt_ln(k)
                    pe_tt.wait(act, it, use)
                    act_tt.inc(copy(xnT[:, k, :], bank(tt, use)[:, :], bias=vcol(LNB + k), scale=vcol(LNG + k)))
                for j in range(FCH):
                    use = mm_gate(j)
                    pe_mm.wait(act, it, use)
                    if j >= 2:
                        done(act, dve_dd, it, dd_a(j - 2))
                    act_mm.inc(nc.scalar.activation(gel[0:FW[j], j % 2, :], bank(mm, use)[0:FW[j], :], ACT.Gelu,
                                                    bias=vec[0:FW[j], B1G + j:B1G + j + 1]))

            loop(act, body)
            for c in (act_mm, act_tt, act_st, xs_used, v_in):
                c.done()

        @block.vector
        def _(dve):
            dve.sem_inc(dve_dd.sem, dve_dd.start)
            dve.sem_inc(qk_in.sem, qk_in.start)
            dve.sem_inc(ffn_out.sem, ffn_out.start)

            def body(l, bt, h, it):
                base = bt * XROW + h * GROUP

                def link(ins):
                    chain.wait(dve, it, chain.inc(ins))

                def rotate(i, chunks):
                    for c in chunks:
                        n = 4 * i + c + 1
                        done(dve, act_mm, it, mm_q(i, c))
                        dst = heads(qk[:, c, :])
                        tab = rotl[:, bass.ds(h * TPG + i, 1), 2 * (c % 2), :]
                        nc.vector.tensor_tensor(dst, heads(raw[:, c, :]), tab.broadcast_to([P, 8, DHEAD]), ALU.mult)
                        link(nc.vector.tensor_reduce(ss[:, c, :], heads(sq[:, c, :]), AX_X, ALU.add))
                        hs = slice(8 * (c // 2), 8 * (c // 2) + 8)
                        ss_in.inc(nc.vector.tensor_scalar(ss[:, c, :], ss[:, c, :], NORM_FLOOR, None, ALU.max))
                        turn_in.wait(dve, it, n)
                        if c % 2 == 0:
                            norm_in.wait(dve, it, n)
                        ins = nc.vector.tensor_tensor(qk[:, c, :], qk[:, c, :], turn[:, c % 2, :], ALU.add)
                        if c % 2 == 1:
                            link(ins)
                            norm_in.wait(dve, it, n)
                            ins = nc.vector.tensor_tensor(dst, dst, kn[:, hs].rearrange("p (h o) -> p h o", o=1).broadcast_to([P, 8, DHEAD]), ALU.mult)
                        qk_in.inc(ins)

                def maxima(i, g):
                    use = HG * i + g + 1
                    hs = slice(HG * g, HG * g + HG)
                    pe_st.wait(dve, it, use)
                    link(nc.vector.tensor_reduce(mx[:, hs], heads(bank(st, use)[:, :], HG), AX_X, ALU.max))
                    nb_in.inc(nc.vector.scalar_tensor_tensor(nb[:, hs], mx[:, hs], -1.0, qn[:, i % 2, head_of(g, 0):head_of(g, HG - 1) + 1:2], ALU.mult, ALU.mult))

                def normalise(i, g):
                    use = HG * i + g + 1
                    hs = slice(HG * g, HG * g + HG)
                    done(dve, act_st, it, use)
                    link(nc.vector.reciprocal(rden[:, hs], den[:, hs]))
                    dst = heads(pr[:, g % 2, :], HG)
                    pr_in.inc(nc.vector.tensor_tensor(dst, dst, rden[:, hs].rearrange("p (h o) -> p h o", o=1).broadcast_to([P, HG, TILE]), ALU.mult))

                def take_o(i, half):
                    use = dd_o(i, half)
                    pe_dd.wait(dve, it, use)
                    dve_dd.inc(nc.vector.tensor_copy(oT[:, 4 * half:4 * half + 4, i * TILE:(i + 1) * TILE],
                                                     bank(dd, use)[:, :].rearrange("p (j t) -> p j t", j=4)))

                dve.wait_ge(rotl_in, l + 1)
                rotate(0, range(4))
                for i in range(TPG):
                    maxima(i, 0)
                    maxima(i, 1)
                    normalise(i, 0)
                    if i + 1 < TPG:
                        rotate(i + 1, (0, 1))
                    maxima(i, 2)
                    normalise(i, 1)
                    if i + 1 < TPG:
                        rotate(i + 1, (2, 3))
                    take_o(i, 0)
                    maxima(i, 3)
                    normalise(i, 2)
                    normalise(i, 3)
                    take_o(i, 1)
                for m in range(KT):
                    use = dd_wo(m)
                    pe_dd.wait(dve, it, use)
                    at = bass.ds(base + m, GROUP)
                    ins = nc.vector.tensor_tensor(xb[:, m, at], bank(dd, use)[:, :], xa[:, m, at], ALU.add)
                    n_out = attn_out.inc(ins)
                    attn_out.wait(dve, it, n_out)
                    dve_dd.n += 1
                    dve.sem_inc(dve_dd.sem, 1)
                for pq in range(TPG // 2):
                    use = dd_ft(pq)
                    pe_dd.wait(dve, it, use)
                    src = bank(dd, use)
                    for i in range(2):
                        link(nc.vector.bn_stats(stats[:, 2 * pq + i, :], src[:, i * DIM:(i + 1) * DIM]))
                    for i in range(2):
                        dve.sem_inc(dve_passed, 1)
                        link(nc.vector.bn_aggr(mv[:, 2 * pq + i, :], stats[:, 2 * pq + i, :]))
                    ts = slice(2 * pq, 2 * pq + 2)
                    var_in.inc(nc.vector.tensor_scalar(mv[:, ts, 1], mv[:, ts, 1], LN_EPS, None, ALU.add))
                    rstd_in.wait(dve, it, pq + 1)
                    for i in range(2):
                        t = 2 * pq + i
                        ins = nc.vector.tensor_scalar(xn[:, t, :], src[:, i * DIM:(i + 1) * DIM], mv[:, t, 0:1], rstd[:, t:t + 1],
                                                      ALU.subtract, ALU.mult)
                    dve_dd.inc(ins)
                dve.wait_ge(vec_in, l + 1)
                for j in range(FCH):
                    use = dd_a(j)
                    pe_dd.wait(dve, it, use)
                    done(dve, act_mm, it, mm_gate(j))
                    w = FW[j]
                    dve_dd.inc(nc.vector.scalar_tensor_tensor(u[0:w, j, :], bank(dd, use)[0:w, :], vec[0:w, B1A + j:B1A + j + 1], gel[0:w, j % 2, :],
                                                              ALU.add, ALU.mult))
                for m in range(KT):
                    use = dd_w2(m)
                    pe_dd.wait(dve, it, use)
                    at = bass.ds(base + m, GROUP)
                    ins = nc.vector.scalar_tensor_tensor(xa[:, m, at], bank(dd, use)[:, :], vcol(B2 + m), xb[:, m, at], ALU.add, ALU.add)
                    n_out = ffn_out.inc(ins)
                    done(dve, ffn_out, it, n_out)
                    dve_dd.n += 1
                    dve.sem_inc(dve_dd.sem, 1)

            loop(dve, body)
            for c in (dve_dd, qk_in, nb_in, pr_in, attn_out, ffn_out, chain):
                c.done()
            dve.wait_ge(final_in, 16)
            xcols = oT[:, :, :].rearrange("p k n -> p (k n)")
            for n in range(KT * BATCH):
                k, bt = n // BATCH, n % BATCH
                at = slice(bt * XROW + k, bt * XROW + k + SEQ)
                nc.vector.tensor_tensor(xa[:, k, at], xa[:, k, at], xcols[:, n * SEQ:(n + 1) * SEQ], ALU.add).then_inc(final_summed, 1)


def rotary_tables(np):
    half = np.arange(0, DHEAD, 2, dtype=np.float32)
    inv_freq = (1.0 / np.float32(10000.0) ** (half / np.float32(DHEAD))).astype(np.float32)
    t = np.arange(SEQ, dtype=np.float32)
    freqs = t[:, None] * inv_freq[None, :]
    freqs = np.concatenate([freqs, freqs], -1)
    base = (half + np.float32(0.4 * DHEAD)) / np.float32(1.4 * DHEAD)
    power = (t - SEQ // 2) / np.float32(WINDOW // 2)
    scale = (base[None, :] ** power[:, None]).astype(np.float32)
    scale = np.concatenate([scale, scale], -1)
    sign = np.concatenate([-np.ones(DHEAD // 2), np.ones(DHEAD // 2)]).astype(np.float32)
    cos, sin = np.cos(freqs), np.sin(freqs) * sign
    return np.stack([QK_SCALE * cos * scale, QK_SCALE * sin * scale, cos / scale, sin / scale], 1).astype(np.float32)


def window_masks(np):
    i, j = np.arange(WINDOW)[:, None], np.arange(WINDOW)[None, :]
    own, before = np.where(j <= i, 0.0, MASKED), np.where(j >= i, 0.0, MASKED)
    none = np.full((WINDOW, WINDOW), MASKED)
    second = np.concatenate([before, own], 1)
    return np.stack([np.concatenate([np.concatenate([own, b], 1), second], 0) for b in (none, before)])


def kernel(x, cond_1024, L0_cond_Wx, L0_cond_Wh, L0_cond_b, L0_ffn_Wqkv, L0_ffn_q_scale, L0_ffn_k_scale, L0_ffn_Wo,
           L0_ffn_ln_g, L0_ffn_ln_b, L0_ffn_W1, L0_ffn_b1, L0_ffn_W2, L0_ffn_b2):
    import ml_dtypes
    import numpy as np
    import concourse.bacc as bacc
    from concourse.bass_utils import run_bass_kernel_spmd

    def rows(w):
        w = np.asarray(w)
        pad = -w.shape[-2] % P
        w = np.concatenate([w, np.zeros((*w.shape[:-2], pad, w.shape[-1]), w.dtype)], -2)
        return np.swapaxes(w.reshape(*w.shape[:-2], -1, P, w.shape[-1]), -3, -2)

    def flat(w):
        return w.reshape(*w.shape[:-2], -1)

    def cols(v):
        return rows(np.asarray(v)[..., None])[..., 0]

    b1 = np.asarray(L0_ffn_b1)
    vecs = np.concatenate([cols(v) for v in (b1[:, :FF], b1[:, FF:], L0_ffn_ln_g, L0_ffn_ln_b, L0_ffn_b2)], -1)
    q_scale, k_scale = np.asarray(L0_ffn_q_scale), np.asarray(L0_ffn_k_scale)
    swap = lambda v: np.roll(v, DHEAD // 2, -1)
    xh = np.asarray(x)
    nc = bacc.Bacc("TRN2", target_bir_lowering=False, num_devices=1)
    given = {
        "x_cols": rows(xh.transpose(2, 0, 1).reshape(DIM, BATCH * SEQ)),
        "h0_cols": flat(rows(np.asarray(cond_1024).T)),
        "Wx": rows(L0_cond_Wx), "Wh": rows(L0_cond_Wh), "b_cols": cols(L0_cond_b),
        "Wqkv": flat(rows(L0_ffn_Wqkv)), "qk_scales": np.concatenate([q_scale, swap(q_scale), k_scale, swap(k_scale)], -1),
        "Wo": flat(rows(L0_ffn_Wo)), "W1": flat(rows(L0_ffn_W1)), "W2": flat(rows(L0_ffn_W2)),
        "layer_vecs": np.swapaxes(vecs, 0, 1),
        "rotary": rotary_tables(np), "masks": window_masks(np).astype(ml_dtypes.bfloat16), "identity": np.eye(P, dtype=np.float32),
    }
    arrays = {f"in_{n}": np.ascontiguousarray(a) for n, a in given.items()}
    args = [nc.dram_tensor(n, a.shape, mybir.dt.from_np(a.dtype), kind="ExternalInput").ap() for n, a in arrays.items()]
    args.append(nc.dram_tensor("out_cols", (P, KT, BATCH * SEQ), F32, kind="ExternalOutput").ap())
    build_program(nc, *args)
    r = run_bass_kernel_spmd(nc, [arrays], core_ids=[0])
    got = np.asarray(r.results[0]["out_cols"])
    return np.ascontiguousarray(got.transpose(1, 0, 2).reshape(DIM, BATCH, SEQ).transpose(1, 2, 0))
```

```python
from contextlib import ExitStack

import concourse.bass as bass
from concourse import mybir

F32 = mybir.dt.float32
BF16 = mybir.dt.bfloat16
ALU = mybir.AluOpType
ACT = mybir.ActivationFunctionType
AX_X = mybir.AxisListType.X

P = 128
BATCH, SEQ, DIM = 2, 1024, 256
KT = DIM // P
DEPTH, HEADS, DHEAD, WINDOW = 6, 16, 64, 64
INNER = HEADS * DHEAD
FF = int(DIM * 4 * 2 / 3)
FCH = (FF + P - 1) // P
FW = [min(P, FF - P * j) for j in range(FCH)]
GATES = 4 * DIM
GM = GATES // P
QK_SCALE = 8.0
LN_EPS = 1e-5
NORM_FLOOR = 1e-24
MASKED = -1.0e30

TILE = 128
CHUNK = 256
CHUNKS = SEQ // CHUNK
GROUP = BATCH * CHUNK
TPG = GROUP // TILE
TPC = CHUNK // TILE
ROW = CHUNK + 1
PARTS = 3
HC = KT * BATCH
XWC = GM * PARTS * BATCH
UNROLL = 4
SLOTS = 42
HALFS = SLOTS // 2
LEAD = SEQ - (CHUNKS - 1) * DEPTH * SLOTS
assert LEAD >= CHUNK and LEAD % UNROLL == 0 and all(LEAD + c * DEPTH * SLOTS >= (c + 1) * CHUNK for c in range(CHUNKS))
CHAIN = TPG * (2 * 1 + 2 * 2 + 4 + 4 + 2)


class Count:

    def __init__(self, sem, per, start=0):
        self.sem, self.per, self.start, self.n = sem, per, start, 0

    def inc(self, ins):
        self.n += 1
        ins.then_inc(self.sem, 1)
        return (self.n - 1) % self.per + 1

    def check(self, passes):
        assert self.n == self.per * passes, (self.sem, self.n, self.per)

    def wait(self, eng, it, n):
        eng.wait_ge(self.sem, it * self.per + n)


def pairs(ap):
    return ap.rearrange("p (a b) -> p a b", b=BATCH)


class Lstm:

    def __init__(self, sb, sem):
        self.whp = sb("whp", [P, PARTS, KT, GATES], BF16)
        self.state = sb("state", [P, 5 * HC])
        self.uv = sb("uv", [P, 2 * HC])
        self.tcell = sb("tcell", [P, HC])
        self.gsum = sb("gsum", [P, GM * BATCH])
        self.h32 = sb("h32", [P, HC])
        self.hrest = sb("hrest", [P, HC])
        self.hp = sb("hp", [P, KT, PARTS, BATCH], BF16)
        self.hist = sb("hist", [P, SEQ, HC])
        self.gates_done, self.gates_summed, self.gates_act = sem("gates_done"), sem("gates_summed"), sem("gates_act")
        self.uv_done, self.cell_done, self.cell_tanh = sem("uv_done"), sem("cell_done"), sem("cell_tanh")
        self.h_hi, self.h_chain, self.h_rest, self.h_parts = sem("h_hi"), sem("h_chain"), sem("h_rest"), sem("h_parts")
        self.history = sem("history")

    def on_pe(self, nc, pe, t, g, ident16, xw_t, others):
        pe.wait_ge(self.gates_summed, t + 2 - others)
        nc.tensor.matmul(g[:, 0:XWC], ident16[:, :], xw_t, start=True, stop=False, skip_group_check=True)
        pe.wait_ge(self.h_hi, t + 1)
        for m in range(GM):
            for k in range(KT):
                nc.tensor.matmul(g[:, m * PARTS * BATCH:m * PARTS * BATCH + BATCH], self.whp[:, 2, k, m * P:(m + 1) * P],
                                 self.hp[:, k, 0, :], start=False, stop=False, skip_group_check=True)
        pe.wait_ge(self.h_parts, t + 1)
        for m in range(GM):
            for p in (1, 0):
                for k in range(KT):
                    last = nc.tensor.matmul(g[:, m * PARTS * BATCH:(m + 1) * PARTS * BATCH], self.whp[:, p, k, m * P:(m + 1) * P],
                                            self.hp[:, k, :, :].rearrange("p a b -> p (a b)"), start=False, stop=(m == GM - 1),
                                            skip_group_check=True)
        last.then_inc(self.gates_done, 1)

    def on_act(self, nc, act, t):
        act.wait_ge(self.gates_summed, t + 3)
        nc.scalar.activation(self.state[:, 0:4 * HC], self.gsum[:, :], ACT.Tanh).then_inc(self.gates_act, 1)
        act.wait_ge(self.cell_done, t + 1)
        nc.scalar.activation(self.tcell[:, :], self.state[:, 4 * HC:5 * HC], ACT.Tanh, scale=0.5).then_inc(self.cell_tanh, 1)

    def on_dve(self, nc, dve, t, g):
        state, uv, hp, h32 = self.state, self.uv, self.hp, self.h32
        dve.wait_ge(self.gates_done, t + 1)
        nc.vector.tensor_reduce(self.gsum[:, :].rearrange("p (m b) -> p m b", b=BATCH),
                                g[:, 0:XWC].rearrange("p (m q b) -> p m b q", q=PARTS, b=BATCH), AX_X, ALU.add).then_inc(self.gates_summed, 1)
        dve.wait_ge(self.gates_act, t + 1)
        nc.vector.scalar_tensor_tensor(uv[:, :], state[:, 0:2 * HC], 1.0, state[:, 3 * HC:5 * HC], ALU.add, ALU.mult).then_inc(self.uv_done, 1)
        dve.wait_ge(self.uv_done, t + 1)
        nc.vector.scalar_tensor_tensor(state[:, 4 * HC:5 * HC], uv[:, HC:2 * HC], 0.5, uv[:, 0:HC], ALU.mult, ALU.add).then_inc(self.cell_done, 1)
        dve.wait_ge(self.cell_tanh, t + 1)
        nc.vector.scalar_tensor_tensor(hp[:, :, 0, :], pairs(state[:, 2 * HC:3 * HC]), 1.0, pairs(self.tcell[:, :]), ALU.add, ALU.mult).then_inc(self.h_hi, 1)
        nc.vector.scalar_tensor_tensor(h32[:, :], state[:, 2 * HC:3 * HC], 1.0, self.tcell[:, :], ALU.add, ALU.mult).then_inc(self.h_chain, 1)
        dve.wait_ge(self.h_hi, t + 2)
        dve.wait_ge(self.h_chain, 2 * t + 1)
        nc.vector.tensor_tensor(hp[:, :, 1, :], pairs(h32[:, :]), hp[:, :, 0, :], ALU.subtract).then_inc(self.h_chain, 1)
        nc.vector.tensor_tensor(pairs(self.hrest[:, :]), pairs(h32[:, :]), hp[:, :, 0, :], ALU.subtract).then_inc(self.h_rest, 1)
        dve.wait_ge(self.h_chain, 2 * t + 2)
        dve.wait_ge(self.h_rest, t + 1)
        nc.vector.tensor_tensor(hp[:, :, 2, :], pairs(self.hrest[:, :]), hp[:, :, 1, :], ALU.subtract).then_inc(self.h_parts, 1)
        nc.vector.tensor_scalar(self.hist[:, bass.ds(t, 1), :].rearrange("p a n -> p (a n)"), h32[:, :], 0.5, None, ALU.mult).then_inc(self.history, 1)


def build_program(nc, x_cols, h0_cols, Wx, Wh, b_cols, Wqkv, qk_scales, Wo, W1, W2, layer_vecs, rotary, masks, identity, out):
    with ExitStack() as ctx:
        def sb(name, shape, dt=F32, c=ctx):
            return c.enter_context(nc.sbuf_tensor(name, shape, dt))

        def sem(name, c=ctx):
            return c.enter_context(nc.semaphore(name))

        ident = sb("ident", [P, P])
        ident16 = sb("ident16", [P, P], BF16)
        vecs = sb("vecs", [P, DEPTH, 2 * FCH + 3 * KT])
        wqkv = sb("wqkv", [P, KT * 3 * INNER])
        wo = sb("wo", [P, INNER // P * DIM])
        w1 = sb("w1", [P, KT * 2 * FF])
        w2 = sb("w2", [P, FCH * DIM])
        weights = [(w, src, sem(f"w_in{n}")) for n, (w, src) in enumerate(((wqkv, Wqkv), (wo, Wo), (w1, W1), (w2, W2)))]
        lstm = Lstm(sb, sem)
        xw_dram = nc.dram_tensor("xw_parts", (P, (SEQ + SLOTS) * XWC), BF16, kind="Internal").ap()
        k_dram = nc.dram_tensor("k_windows", (DEPTH, BATCH, P, HEADS // 2 * WINDOW), F32, kind="Internal").ap()
        v_dram = nc.dram_tensor("v_windows", (DEPTH, BATCH, WINDOW, INNER), F32, kind="Internal").ap()
        lstm_stage(nc, sb, sem, lstm, x_cols, h0_cols, Wx, Wh, b_cols, layer_vecs, identity, ident, ident16, vecs, weights,
                   xw_dram, k_dram, v_dram)
        layer_stage(nc, sb, sem, lstm, x_cols, qk_scales, rotary, masks, ident, ident16, vecs, weights, xw_dram, k_dram, v_dram, out)


def lstm_stage(nc, sb0, sem0, lstm, x_cols, h0_cols, Wx, Wh, b_cols, layer_vecs, identity, ident, ident16, vecs, weights,
               xw_dram, k_dram, v_dram):
    with ExitStack() as ctx:
        def sb(name, shape, dt=F32):
            return sb0(name, shape, dt, ctx)

        def sem(name):
            return sem0(name, ctx)

        xw = sb("xw", [P, SEQ, XWC], BF16)
        wh32 = sb("wh32", [P, KT, GATES])
        wx_sb = sb("wx_sb", [P, KT, GATES])
        xT = sb("xT", [P, KT, BATCH * SEQ])
        bias = sb("bias", [P, GM])
        scratch = lstm.hist[:, :, :].rearrange("p t n -> p (t n)")
        part32 = scratch[:, 0:1024].rearrange("p (a n) -> p a n", a=2)
        rest32 = scratch[:, 1024:1536]
        zero = scratch[:, SEQ * HC - INNER:SEQ * HC]
        assert LEAD * HC <= SEQ * HC - INNER
        whp, hp, h32, hrest = lstm.whp, lstm.hp, lstm.h32, lstm.hrest
        ps = [ctx.enter_context(nc.psum_tensor(f"gates{i}", [P, 512], F32)) for i in range(2)]

        const_in, wx_in, wh_in, h0_in, xt_in = sem("const_in"), sem("wx_in"), sem("wh_in"), sem("h0_in"), sem("xt_in")
        zeroed, prep, spilled = sem("zeroed"), sem("prep"), sem("spilled")
        projected, xw_evac, xw_split, xw_chain = sem("projected"), sem("xw_evac"), sem("xw_split"), sem("xw_chain")
        NP = GM * BATCH * SEQ // 512

        block = ctx.enter_context(nc.Block("lstm"))

        @block.sync
        def _(sp):
            sp.dma_start(wx_sb[:, :, :], Wx).then_inc(wx_in, 16)
            sp.dma_start(xT[:, :, :], x_cols).then_inc(xt_in, 16)
            sp.dma_start(bias[:, :], b_cols).then_inc(h0_in, 16)
            sp.dma_start(h32[:, :], h0_cols).then_inc(h0_in, 16)
            sp.dma_start(ident[:, :], identity).then_inc(const_in, 16)
            sp.dma_start(vecs[:, :, :], layer_vecs).then_inc(const_in, 16)
            sp.dma_start(wh32[:, :, :], Wh).then_inc(wh_in, 16)
            for w, src, landed in weights:
                sp.dma_start(w[:, :], src[0, :, :]).then_inc(landed, 16)
            sp.wait_ge(zeroed, 2)
            for l in range(DEPTH):
                for bt in range(BATCH):
                    sp.dma_start(k_dram[l, bt, :, :], zero[:, 0:HEADS // 2 * WINDOW]).then_inc(spilled, 16)
                    sp.dma_start(v_dram[l, bt, :, :], zero[0:WINDOW, :]).then_inc(spilled, 16)
            sp.wait_ge(xw_split, NP)
            sp.dma_start(xw_dram[:, LEAD * XWC:SEQ * XWC], xw[:, LEAD:SEQ, :].rearrange("p t n -> p (t n)")).then_inc(spilled, 16)
            sp.dma_start(xw_dram[:, SEQ * XWC:(SEQ + SLOTS) * XWC], xw[:, 0:SLOTS, :].rearrange("p t n -> p (t n)")).then_inc(spilled, 16)
            sp.wait_ge(spilled, 16 * (2 * DEPTH * BATCH + 2))

        @block.gpsimd
        def _(pool):
            nc.gpsimd.memset(lstm.state[:, :], 0.0).then_inc(zeroed, 1)
            nc.gpsimd.memset(zero, 0.0).then_inc(zeroed, 1)

        @block.tensor
        def _(pe):
            pe.wait_ge(xt_in, 16)
            pe.wait_ge(wx_in, 16)
            n = 0
            for m in range(GM):
                for c in range(BATCH * SEQ // 512):
                    if n >= 2:
                        pe.wait_ge(xw_evac, n - 1)
                    for k in range(KT):
                        last = nc.tensor.matmul(ps[n % 2][:, :], wx_sb[:, k, m * P:(m + 1) * P], xT[:, k, c * 512:(c + 1) * 512],
                                                start=(k == 0), stop=(k == KT - 1))
                    last.then_inc(projected, 1)
                    n += 1
            pe.wait_ge(xw_split, n)
            pe.wait_ge(prep, 2)
            with pe.Fori(0, LEAD // UNROLL) as it:
                for s in range(UNROLL):
                    lstm.on_pe(nc, pe, it * UNROLL + s, ps[s % 2], ident16, xw[:, it * UNROLL + s, :], 1)

        @block.scalar
        def _(act):
            act.wait_ge(prep, 1)
            n = 0
            for m in range(GM):
                for c in range(BATCH * SEQ // 512):
                    act.wait_ge(projected, n + 1)
                    if n >= 2:
                        act.wait_ge(xw_split, n - 1)
                    nc.scalar.activation(part32[:, n % 2, :], ps[n % 2][:, :], ACT.Identity, bias=bias[:, m:m + 1],
                                         scale=0.5 if m < 3 * GM // 4 else 1.0).then_inc(xw_evac, 1)
                    n += 1
            with act.Fori(0, LEAD // UNROLL) as it:
                for s in range(UNROLL):
                    lstm.on_act(nc, act, it * UNROLL + s)

        @block.vector
        def _(dve):
            n_chain = [0]

            def link(ins):
                n_chain[0] += 1
                ins.then_inc(xw_chain, 1)
                dve.wait_ge(xw_chain, n_chain[0])

            dve.wait_ge(h0_in, 32)
            nc.vector.tensor_scalar(bias[:, 0:3 * GM // 4], bias[:, 0:3 * GM // 4], 0.5, None, ALU.mult).then_inc(prep, 1)
            dve.wait_ge(const_in, 32)
            link(nc.vector.tensor_copy(ident16[:, :], ident[:, :]))
            dve.wait_ge(wh_in, 16)
            for k in range(KT):
                for c in range(GATES // 512):
                    cols = slice(c * 512, (c + 1) * 512)
                    w = wh32[:, k, cols]
                    sig = min(512, 3 * DIM - c * 512)
                    link(nc.vector.tensor_scalar(w[:, 0:sig], w[:, 0:sig], 0.25, None, ALU.mult))
                    if sig < 512:
                        link(nc.vector.tensor_scalar(w[:, sig:512], w[:, sig:512], 0.5, None, ALU.mult))
                    link(nc.vector.tensor_copy(whp[:, 0, k, cols], w))
                    link(nc.vector.tensor_tensor(w, w, whp[:, 0, k, cols], ALU.subtract))
                    link(nc.vector.tensor_copy(whp[:, 1, k, cols], w))
                    link(nc.vector.tensor_tensor(whp[:, 2, k, cols], w, whp[:, 1, k, cols], ALU.subtract))
            link(nc.vector.tensor_scalar(h32[:, :], h32[:, :], 2.0, None, ALU.mult))
            link(nc.vector.tensor_copy(hp[:, :, 0, :], pairs(h32[:, :])))
            link(nc.vector.tensor_tensor(pairs(hrest[:, :]), pairs(h32[:, :]), hp[:, :, 0, :], ALU.subtract))
            link(nc.vector.tensor_copy(hp[:, :, 1, :], pairs(hrest[:, :])))
            link(nc.vector.tensor_tensor(hp[:, :, 2, :], pairs(hrest[:, :]), hp[:, :, 1, :], ALU.subtract))
            n = 0
            for m in range(GM):
                for c in range(BATCH * SEQ // 512):
                    bb, t0 = c // (SEQ // 512), (c % (SEQ // 512)) * 512
                    dve.wait_ge(xw_evac, n + 1)
                    src = part32[:, n % 2, :]
                    at = [xw[:, t0:t0 + 512, (m * PARTS + q) * BATCH + bb] for q in range(PARTS)]
                    link(nc.vector.tensor_copy(at[0], src))
                    link(nc.vector.tensor_tensor(rest32, src, at[0], ALU.subtract))
                    link(nc.vector.tensor_copy(at[1], rest32))
                    ins = nc.vector.tensor_tensor(at[2], rest32, at[1], ALU.subtract)
                    ins.then_inc(xw_split, 1)
                    dve.wait_ge(xw_split, n + 1)
                    n += 1
            dve.wait_ge(zeroed, 2)
            dve.sem_inc(lstm.gates_summed, 2)
            dve.sem_inc(lstm.h_hi, 1)
            dve.sem_inc(lstm.h_parts, 1)
            dve.sem_inc(prep, 1)
            with dve.Fori(0, LEAD // UNROLL) as it:
                for s in range(UNROLL):
                    lstm.on_dve(nc, dve, it * UNROLL + s, ps[s % 2])


def layer_stage(nc, sb0, sem0, lstm, x_cols, qk_scales, rotary, masks, ident, ident16, vecs, weights, xw_dram, k_dram, v_dram, out):
    with ExitStack() as ctx:
        def sb(name, shape, dt=F32):
            return sb0(name, shape, dt, ctx)

        def sem(name):
            return sem0(name, ctx)

        HALF = DHEAD // 2
        HG = 4
        (wqkv_, wqkv_src, wqkv_in), (wo_, wo_src, wo_in), (w1_, w1_src, w1_in), (w2_, w2_src, w2_in) = weights
        wqkv = wqkv_[:, :].rearrange("p (k n) -> p k n", k=KT)
        wo = wo_[:, :].rearrange("p (k n) -> p k n", n=DIM)
        w1 = w1_[:, :].rearrange("p (k n) -> p k n", k=KT)
        w2 = w2_[:, :].rearrange("p (k n) -> p k n", n=DIM)
        xa = sb("xa", [P, KT, BATCH, ROW])
        xb = sb("xb", [P, KT, BATCH, ROW])
        edge_a = sb("edge_a", [P, DEPTH, BATCH])
        edge_b = sb("edge_b", [P, DEPTH, BATCH])
        xres = sb("xres", [P, KT, GROUP])
        xwp = sb("xwp", [P, SLOTS, XWC], BF16)
        rot = sb("rot", [P, CHUNKS * TPC, 4 * DHEAD])
        rotl = sb("rotl", [P, TPC, 4, DHEAD])
        scales = sb("scales", [P, 4 * DHEAD])
        mask = sb("mask", [P, CHUNKS, TILE], BF16)
        vec = sb("vec", [P, 2 * FCH + 3 * KT])
        raw = sb("raw", [P, 4, 512])
        sq = sb("sq", [P, 4, 512])
        qk = sb("qk", [P, 4, 512])
        turn = sb("turn", [P, 2, 512])
        ss = sb("ss", [P, 4, 8])
        qn = sb("qn", [P, 2, HEADS])
        kn = sb("kn", [P, HEADS])
        power = sb("power", [P, 8])
        va = sb("va", [P, 2, INNER])
        vb = sb("vb", [P, 2, INNER])
        qT = sb("qT", [P, HEADS // 2, TILE])
        kT = sb("kT", [P, 2, HEADS // 2, 3 * WINDOW])
        mx = sb("mx", [P, HEADS])
        nb = sb("nb", [P, HEADS])
        den = sb("den", [P, HEADS])
        rden = sb("rden", [P, HEADS])
        u = sb("u", [P, FCH, GROUP])
        pr, pT = u[:, 0:2, :], u[:, 2:4, :]
        oT = sb("oT", [P, INNER // P, GROUP])
        stats = sb("stats", [P, TPG, 6])
        mv = sb("mv", [P, TPG, 2])
        rstd = sb("rstd", [P, TPG])
        xn = sb("xn", [P, TPG, DIM])
        xnT = sb("xnT", [P, KT, GROUP])
        gel = sb("gel", [P, 2, GROUP])

        def pb(name):
            return ctx.enter_context(nc.psum_tensor(name, [P, 512], F32))

        mm = [pb("mm0"), pb("mm1")]
        dd = [pb("dd")]
        tt = [pb("tt0"), pb("tt1")]
        st = [pb("st0"), pb("st1")]
        gates = pb("gates")

        sc_in, cst_in, cleared = sem("scales_in"), sem("cst_in"), sem("cleared")
        xres_in, xres_sum, out_done = sem("xres_in"), sem("xres_sum"), sem("out_done")
        xw_in = [sem("xw_in0"), sem("xw_in1")]
        kept_in, kept_out = sem("kept_in"), sem("kept_out")
        chunk_in, rotl_in, vec_in = sem("chunk_in"), sem("rotl_in"), sem("vec_in")
        pool_passed, dve_passed, sp_passed = sem("pool_passed"), sem("dve_passed"), sem("sp_passed")

        pe_mm = Count(sem("pe_mm"), 6 * TPG + FCH)
        act_mm = Count(sem("act_mm"), 6 * TPG + FCH, 2)
        pe_dd = Count(sem("pe_dd"), 2 * TPG + FCH)
        dve_dd = Count(sem("dve_dd"), 2 * TPG + FCH, 1)
        pe_tt = Count(sem("pe_tt"), 8 * TPG + KT)
        act_tt = Count(sem("act_tt"), 8 * TPG + KT, 2)
        pe_st = Count(sem("pe_st"), HG * TPG)
        act_st = Count(sem("act_st"), HG * TPG, 2)
        pe_out = Count(sem("pe_out"), BATCH * KT + KT)
        ss_in = Count(sem("ss_in"), 4 * TPG)
        norm_in = Count(sem("norm_in"), 4 * TPG)
        var_in = Count(sem("var_in"), BATCH)
        rstd_in = Count(sem("rstd_in"), BATCH)
        pe_ft = Count(sem("pe_ft"), BATCH)
        xn_in = Count(sem("xn_in"), BATCH)
        turn_in = Count(sem("turn_in"), 4 * TPG)
        qk_in = Count(sem("qk_in"), 4 * TPG, 4)
        nb_in = Count(sem("nb_in"), HG * TPG)
        pr_in = Count(sem("pr_in"), HG * TPG)
        v_in = Count(sem("v_in"), 2 * TPG)
        vup_in = Count(sem("vup_in"), 2)
        chain = Count(sem("dve_chain"), CHAIN)
        edge_a_in = Count(sem("edge_a_in"), 2)
        edge_b_in = Count(sem("edge_b_in"), 2)
        attn_out = Count(sem("attn_out"), BATCH * KT)
        ffn_out = Count(sem("ffn_out"), KT, KT)

        def mm_q(i, c): return 6 * i + c + 1
        def mm_gate(j): return 6 * TPG + j + 1
        def dd_o(i, half): return 2 * i + half + 1
        def dd_a(j): return 2 * TPG + j + 1
        TURNS = [("qk", 0, 0), ("qk", 0, 1)]
        for i in range(TPG):
            TURNS += [("p", i - 1, 3)] * (i > 0) + [("qk", i, 2), ("qk", i, 3), ("p", i, 0), ("p", i, 1)]
            TURNS += [("qk", i + 1, 0), ("qk", i + 1, 1)] * (i + 1 < TPG) + [("p", i, 2)]
        TURNS += [("p", TPG - 1, 3)]
        def tt_qk(i, c): return TURNS.index(("qk", i, c)) + 1
        def tt_p(i, g): return TURNS.index(("p", i, g)) + 1
        def tt_ln(k): return 8 * TPG + k + 1

        def bank(banks, use): return banks[(use - 1) % len(banks)]

        def freed(eng, sem_, it, use):
            sem_.wait(eng, it, use)

        def done(eng, sem_, it, use):
            sem_.wait(eng, it, use + sem_.start)

        def head_of(g, n):
            return 8 * (g // 2) + g % 2 + 2 * n

        def vcol(j, n=1): return vec[:, j:j + n]
        B1A, B1G, LNG, LNB, B2 = 0, FCH, 2 * FCH, 2 * FCH + KT, 2 * FCH + 2 * KT

        def heads(ap, n=8): return ap.rearrange("p (h d) -> p h d", h=n)

        def columns(buf, i, k, shifted):
            c0 = (i % TPC) * TILE + (0 if shifted else k)
            return buf[:, k, i // TPC, c0:c0 + TILE]

        def tokens(buf, m):
            return buf[:, m, :, m:m + CHUNK]

        def by_batch(ap): return ap.rearrange("p (b t) -> p b t", b=BATCH)

        def step(it, slot): return it * SLOTS + (LEAD + slot)

        def passes(eng, body, chunk_start=None, chunk_end=None):
            with eng.Fori(0, CHUNKS - 1) as c:
                if chunk_start:
                    chunk_start(c)
                with eng.Fori(0, DEPTH) as l:
                    body(c, l, c * DEPTH + l, True)
                if chunk_end:
                    chunk_end(c)
            c = CHUNKS - 1
            if chunk_start:
                chunk_start(c)
            with eng.Fori(0, DEPTH) as l:
                body(c, l, l + c * DEPTH, False)
            if chunk_end:
                chunk_end(c)

        NCLEAR = 5
        COUNTS = [v for v in locals().values() if isinstance(v, Count)]

        block = ctx.enter_context(nc.Block("layers"))

        @block.sync
        def _(sp):
            def passed():
                sp.sem_inc(sp_passed, 1)

            def load_kept(l, bt):
                passed()
                sp.dma_start(kT[:, 0, :, 2 * WINDOW:3 * WINDOW],
                             k_dram[bass.ds(l, 1), bt, :, :].rearrange("a p (j t) -> p (a j) t", t=WINDOW)).then_inc(kept_in, 16)
                sp.dma_start(va[WINDOW:P, 0, :], v_dram[bass.ds(l, 1), bt, :, :].rearrange("a p n -> (a p) n")).then_inc(kept_in, 16)

            def store_kept(l, bt):
                passed()
                sp.dma_start(k_dram[bass.ds(l, 1), bt, :, :].rearrange("a p (j t) -> p (a j) t", t=WINDOW),
                             kT[:, 1, :, WINDOW:2 * WINDOW]).then_inc(kept_out, 16)
                sp.dma_start(v_dram[bass.ds(l, 1), bt, :, :].rearrange("a p n -> (a p) n"), vb[WINDOW:P, 1, :]).then_inc(kept_out, 16)

            def load_weight(n, l):
                passed()
                w, src, landed = weights[n]
                sp.dma_start(w[:, :], src[bass.ds(l, 1), :, :].rearrange("a p n -> (a p) n")).then_inc(landed, 16)

            def load_scales(l):
                passed()
                sp.dma_start(scales[:, :], qk_scales[bass.ds(l, 1), :].partition_broadcast(P).rearrange("p a n -> p (a n)")).then_inc(sc_in, 16)

            def load_xw(n, step0):
                passed()
                sp.dma_start(xwp[:, n * HALFS:(n + 1) * HALFS, :].rearrange("p t n -> p (t n)"),
                             xw_dram[:, bass.ds(step0 * XWC, HALFS * XWC)]).then_inc(xw_in[n], 16)

            def body(c, l, it, recur, nxt):
                sp.wait_ge(kept_out, it * 64 + 32)
                passed()
                pe_dd.wait(sp, it, dd_o(0, 1))
                load_kept(l, 1)
                done(sp, act_tt, it, tt_qk(1, 3))
                passed()
                v_in.wait(sp, it, 4)
                store_kept(l, 0)
                sp.wait_ge(rotl_in, it + 1)
                load_scales(nxt)
                pe_mm.wait(sp, it, mm_q(TPG - 1, 5))
                load_weight(0, nxt)
                pe_dd.wait(sp, it, dd_o(2, 1))
                load_kept(nxt, 0)
                done(sp, act_tt, it, tt_qk(3, 3))
                passed()
                v_in.wait(sp, it, 8)
                store_kept(l, 1)
                if recur:
                    sp.wait_ge(lstm.gates_done, step(it, HALFS))
                    load_xw(0, step(it, SLOTS))
                pe_out.wait(sp, it, BATCH * KT)
                load_weight(1, nxt)
                pe_dd.wait(sp, it, dd_a(FCH - 1))
                load_weight(2, nxt)
                pe_out.wait(sp, it, BATCH * KT + KT)
                load_weight(3, nxt)
                if recur:
                    sp.wait_ge(lstm.gates_done, step(it, SLOTS))
                    load_xw(1, step(it, SLOTS + HALFS))

            sp.dma_start(mask[:, :, :], masks.rearrange("a p n -> p a n")).then_inc(cst_in, 16)
            sp.dma_start(rot[:, :, :].rearrange("p t (a d) -> p t a d", a=4), rotary.rearrange("(t p) a d -> p t a d", p=P)).then_inc(cst_in, 16)
            load_scales(0)
            sp.wait_ge(cleared, NCLEAR)
            load_kept(0, 0)
            load_xw(0, LEAD)
            load_xw(1, LEAD + HALFS)
            sp.sem_inc(kept_out, 32)

            def chunk(c, recur):
                sp.wait_ge(out_done, c * 16 + 16)
                passed()
                sp.dma_start(xres[:, :, :].rearrange("p k (b t) -> p k b t", b=BATCH),
                             x_cols.rearrange("p k (b t) -> p k b t", b=BATCH)[:, :, :, bass.ds(c * CHUNK, CHUNK)]).then_inc(xres_in, 16)
                with sp.Fori(0, DEPTH - 1) as l:
                    body(c, l, l + c * DEPTH, recur, l + 1)
                body(c, DEPTH - 1, c * DEPTH + (DEPTH - 1), recur, 0)
                sp.wait_ge(xres_sum, (c + 1) * KT)
                passed()
                sp.dma_start(out.rearrange("p k (b t) -> p k b t", b=BATCH)[:, :, :, bass.ds(c * CHUNK, CHUNK)],
                             xres[:, :, :].rearrange("p k (b t) -> p k b t", b=BATCH)).then_inc(out_done, 16)

            with sp.Fori(0, CHUNKS - 1) as c:
                chunk(c, True)
            chunk(CHUNKS - 1, False)
            sp.wait_ge(out_done, (CHUNKS + 1) * 16)
            sp.wait_ge(kept_out, CHUNKS * DEPTH * 64 + 32)

        @block.gpsimd
        def _(pool):
            nc.gpsimd.memset(edge_a[:, :, :], 0.0).then_inc(cleared, 1)
            nc.gpsimd.memset(edge_b[:, :, :], 0.0).then_inc(cleared, 1)
            nc.gpsimd.memset(power[:, :], -0.5).then_inc(cleared, 1)
            nc.gpsimd.memset(kT[:, :, :, :], 0.0).then_inc(cleared, 1)
            nc.gpsimd.memset(va[:, :, :], 0.0).then_inc(cleared, 1)
            pool.wait_ge(cleared, NCLEAR)
            pool.wait_ge(cst_in, 32)

            def passed():
                pool.sem_inc(pool_passed, 1)

            def edge_to(buf, edge, l, count, it):
                passed()
                count.wait(pool, it, count.inc(nc.gpsimd.tensor_copy(buf[:, 1, :, 0:1].rearrange("p b t -> p (b t)"),
                                                                     edge[:, bass.ds(l, 1), :].rearrange("p a b -> p (a b)"))))

            def edge_from(buf, edge, l, count):
                passed()
                count.inc(nc.gpsimd.tensor_copy(edge[:, bass.ds(l, 1), :].rearrange("p a b -> p (a b)"),
                                                buf[:, 1, :, ROW - 1:ROW].rearrange("p b t -> p (b t)")))

            def turns(i, it):
                for c in range(4):
                    use = 4 * i + c + 1
                    done(pool, act_mm, it, mm_q(i, c))
                    qk_in.wait(pool, it, use + 2)
                    src = raw[:, c, :].rearrange("p (h a d) -> p h a d", a=2, d=HALF)
                    dst = turn[:, c % 2, :].rearrange("p (h a d) -> p h a d", a=2, d=HALF)
                    tab = rotl[:, i % TPC, 2 * (c % 2) + 1:2 * (c % 2) + 2, :].rearrange("p o (a d) -> p o a d", a=2)
                    for a in range(2):
                        ins = nc.gpsimd.tensor_tensor(dst[:, :, a, :], src[:, :, 1 - a, :],
                                                      tab[:, :, a, :].broadcast_to([P, 8, HALF]), ALU.mult)
                    turn_in.inc(ins)
                    ss_in.wait(pool, it, use)
                    hs = slice(8 * (c // 2), 8 * (c // 2) + 8)
                    norm_in.inc(nc.gpsimd.tensor_tensor(qn[:, i % 2, hs] if c % 2 == 0 else kn[:, hs], ss[:, c, :], power[:, 0:8], ALU.pow))

            def values_up(i, it):
                v_in.wait(pool, it, 2 * i + 2)
                if i == 0:
                    ffn_out.wait(pool, it, KT)
                else:
                    pe_dd.wait(pool, it, dd_o(i - 1, 1))
                norm_in.wait(pool, it, 4 if i == 0 else 4 * TPG)
                passed()
                vup_in.wait(pool, it, vup_in.inc(nc.gpsimd.tensor_copy(va[WINDOW:P, 1, :], vb[WINDOW:P, 0, :])))

            def body(c, l, it, recur):
                pool.wait_ge(sc_in, (it + 1) * 16)
                done(pool, qk_in, it, 0)
                passed()
                nc.gpsimd.tensor_tensor(rotl[:, :, :, :].rearrange("p t a d -> p t (a d)"), rot[:, bass.ds(c * TPC, TPC), :],
                                        scales[:, :].rearrange("p (o n) -> p o n", o=1).broadcast_to([P, TPC, 4 * DHEAD]),
                                        ALU.mult).then_inc(rotl_in, 1)
                pool.wait_ge(chunk_in, c + 1)
                ffn_out.wait(pool, it, KT)
                edge_to(xa, edge_a, l, edge_a_in, it)
                edge_from(xa, edge_a, l, edge_a_in)
                edge_to(xb, edge_b, l, edge_b_in, it)
                nc.gpsimd.tensor_copy(vec[:, :], vecs[:, bass.ds(l, 1), :].rearrange("p a n -> p (a n)")).then_inc(vec_in, 1)
                pool.wait_ge(rotl_in, it + 1)
                turns(0, it)
                values_up(0, it)
                turns(1, it)
                turns(2, it)
                turns(3, it)
                values_up(2, it)
                for b in range(BATCH):
                    var_in.wait(pool, it, b + 1)
                    ts = slice(TPC * b, TPC * b + TPC)
                    rstd_in.inc(nc.gpsimd.tensor_tensor(rstd[:, ts], mv[:, ts, 1], power[:, 0:TPC], ALU.pow))
                attn_out.wait(pool, it, BATCH * KT)
                edge_from(xb, edge_b, l, edge_b_in)

            passes(pool, body)

        @block.tensor
        def _(pe):
            pe.wait_ge(cleared, NCLEAR)
            pe.wait_ge(cst_in, 32)

            def body(c, l, it, recur):
                slot = [0]

                def lstm_step():
                    if recur:
                        n = slot[0]
                        slot[0] += 1
                        if n % HALFS == 0:
                            pe.wait_ge(xw_in[n // HALFS], (it + 1) * 16)
                        lstm.on_pe(nc, pe, step(it, n), gates, ident16, xwp[:, n, :], 0)

                def project(i, chunks):
                    for c_ in chunks:
                        col = (c_ // 2) * 512 + (c_ % 2) * INNER if c_ < 4 else 2 * INNER + (c_ - 4) * 512
                        use = mm_q(i, c_)
                        freed(pe, act_mm, it, use)
                        for k in range(KT):
                            last = nc.tensor.matmul(bank(mm, use)[:, :], columns(xa, i, k, True), wqkv[:, k, col:col + 512],
                                                    start=(k == 0), stop=(k == KT - 1))
                        pe_mm.inc(last)

                def turn_qk(i, chunks):
                    for c_ in chunks:
                        use = tt_qk(i, c_)
                        done(pe, qk_in, it, 4 * i + c_ + 1)
                        freed(pe, act_tt, it, use)
                        for j in range(4):
                            last = nc.tensor.transpose(bank(tt, use)[:, j * TILE:(j + 1) * TILE], qk[:, c_, j * P:(j + 1) * P], ident[:, :])
                        pe_tt.inc(last)

                def scores(i, g):
                    use = HG * i + g + 1
                    freed(pe, act_st, it, use)
                    done(pe, act_tt, it, tt_qk(i, 1 if g < 2 else 3))
                    if i % TPC == 0 and g == 0:
                        pe.wait_ge(kept_in, it * 64 + (32 if i == 0 else 64))
                    which = c if i % TPC == 0 else 1
                    bk = bank(st, use)
                    nc.tensor.matmul(bk[:, :].rearrange("p (g n) -> p g n", g=HG), ident16[:, :],
                                     mask[:, bass.ds(which, 1), :].broadcast_to([P, HG, TILE]), start=True, stop=False, skip_group_check=True)
                    for w in range(2):
                        for n in range(HG):
                            pair, lo = 4 * (g // 2) + n, DHEAD * (g % 2)
                            keys = kT[lo:lo + DHEAD, i % 2, pair, :].rearrange("p (c x) -> p c x", x=WINDOW)
                            keys = keys[:, 0:3:2, :] if w == 0 else keys[:, 0:2, :]
                            last = nc.tensor.matmul(bk[w * WINDOW:(w + 1) * WINDOW, n * TILE:(n + 1) * TILE].rearrange("p (c x) -> p c x", x=WINDOW),
                                                    qT[lo:lo + DHEAD, pair, w * WINDOW:(w + 1) * WINDOW], keys,
                                                    start=False, stop=(n == HG - 1), skip_group_check=True)
                    pe_st.inc(last)

                def turn_p(i, g):
                    use = tt_p(i, g)
                    pr_in.wait(pe, it, HG * i + g + 1)
                    freed(pe, act_tt, it, use)
                    for n in range(HG):
                        last = nc.tensor.transpose(bank(tt, use)[:, n * TILE:(n + 1) * TILE], pr[:, g % 2, n * TILE:(n + 1) * TILE], ident[:, :])
                    pe_tt.inc(last)

                def values(i, g):
                    use = dd_o(i, g // 2)
                    if g % 2 == 0:
                        freed(pe, dve_dd, it, use)
                    v_in.wait(pe, it, 2 * i + g // 2 + 1)
                    if i % TPC == 1 and g == 0:
                        vup_in.wait(pe, it, i // TPC + 1)
                    done(pe, act_tt, it, tt_p(i, g))
                    bk = bank(dd, use)
                    for n in range(HG):
                        head = head_of(g, n)
                        lo, col = DHEAD * (g % 2), n * TILE
                        for w, v in ((0, va), (1, vb)):
                            last = nc.tensor.matmul(bk[lo:lo + DHEAD, col + w * WINDOW:col + (w + 1) * WINDOW],
                                                    v[:, i % 2, head * DHEAD:(head + 1) * DHEAD],
                                                    pT[:, g % 2, n * TILE + w * WINDOW:n * TILE + (w + 1) * WINDOW],
                                                    start=True, stop=True, skip_group_check=True)
                    if g % 2 == 1:
                        pe_dd.inc(last)

                pe.wait_ge(chunk_in, c + 1)
                ffn_out.wait(pe, it, KT)
                edge_a_in.wait(pe, it, 1)
                pe.wait_ge(wqkv_in, (it + 1) * 16)
                def through_wo(b):
                    if b == 0:
                        pe.wait_ge(wo_in, (it + 1) * 16)
                        done(pe, act_mm, it, 6 * TPG)
                    done(pe, dve_dd, it, dd_o(TPC * b + TPC - 1, 1))
                    ts = slice(b * CHUNK, (b + 1) * CHUNK)
                    for m in range(KT):
                        for k in range(INNER // P):
                            last = nc.tensor.matmul(mm[m][:, ts], wo[:, k, m * P:(m + 1) * P], oT[:, k, ts],
                                                    start=(k == 0), stop=(k == INNER // P - 1), skip_group_check=True)
                        pe_out.inc(last)
                        if b == 0 and m == 0:
                            yield

                def turn_stream(b):
                    done(pe, act_st, it, HG * TPG - 1 + b)
                    attn_out.wait(pe, it, KT * (b + 1))
                    edge_b_in.wait(pe, it, 1)
                    for i in range(TPC):
                        for k in range(KT):
                            last = nc.tensor.transpose(st[b][:, (i * KT + k) * P:(i * KT + k + 1) * P],
                                                       columns(xb, TPC * b + i, k, True), ident[:, :])
                    pe_ft.inc(last)

                def turn_back(b):
                    xn_in.wait(pe, it, b + 1)
                    for k in range(KT):
                        use = tt_ln(k)
                        if b == 0:
                            freed(pe, act_tt, it, use)
                        for i in range(TPC * b, TPC * b + TPC):
                            last = nc.tensor.transpose(bank(tt, use)[:, i * TILE:(i + 1) * TILE], xn[:, i, k * P:(k + 1) * P], ident[:, :])
                        if b == 1:
                            pe_tt.inc(last)

                project(0, (0, 1))
                lstm_step()
                project(0, (2, 3))
                lstm_step()
                project(0, (4, 5))
                lstm_step()
                project(1, (0,))
                turn_qk(0, (0, 1))
                first_wo = through_wo(0)
                for i in range(TPG):
                    more = i + 1 < TPG
                    lstm_step()
                    scores(i, 0)
                    if i > 0:
                        turn_p(i - 1, 3)
                    if more:
                        project(i + 1, (1,))
                    lstm_step()
                    if i > 0:
                        values(i - 1, 3)
                    turn_qk(i, (2, 3))
                    if more:
                        project(i + 1, (2,))
                    else:
                        next(first_wo)
                    lstm_step()
                    scores(i, 1)
                    turn_p(i, 0)
                    lstm_step()
                    if more:
                        scores(i, 2)
                        values(i, 0)
                        project(i + 1, (3,))
                    else:
                        values(i, 0)
                        next(first_wo, None)
                        lstm_step()
                        scores(i, 2)
                    turn_p(i, 1)
                    lstm_step()
                    values(i, 1)
                    if more:
                        turn_qk(i + 1, (0, 1))
                        project(i + 1, (4,))
                    lstm_step()
                    scores(i, 3)
                    turn_p(i, 2)
                    if more:
                        project(i + 1, (5,))
                    lstm_step()
                    values(i, 2)
                    if i + 2 < TPG:
                        project(i + 2, (0,))
                turn_stream(0)
                turn_p(TPG - 1, 3)
                lstm_step()
                values(TPG - 1, 3)
                lstm_step()
                for _ in through_wo(1):
                    pass
                lstm_step()
                turn_back(0)
                turn_stream(1)
                lstm_step()
                lstm_step()
                turn_back(1)
                pe.wait_ge(w1_in, (it + 1) * 16)
                done(pe, act_tt, it, tt_ln(KT - 1))
                for j in range(FCH):
                    for use, bk, src, cnt, col in ((mm_gate(j), mm, act_mm, pe_mm, FF), (dd_a(j), dd, dve_dd, pe_dd, 0)):
                        freed(pe, src, it, use)
                        for k in range(KT):
                            last = nc.tensor.matmul(bank(bk, use)[0:FW[j], :], w1[:, k, col + j * P:col + j * P + FW[j]], xnT[:, k, :],
                                                    start=(k == 0), stop=(k == KT - 1))
                        cnt.inc(last)
                    if j > 0:
                        lstm_step()
                pe.wait_ge(w2_in, (it + 1) * 16)
                done(pe, act_mm, it, mm_gate(FCH - 1))
                done(pe, dve_dd, it, dd_a(FCH - 1))
                for m in range(KT):
                    for k in range(FCH):
                        last = nc.tensor.matmul(mm[m][:, :], w2[0:FW[k], k, m * P:(m + 1) * P], u[0:FW[k], k, :],
                                                start=(k == 0), stop=(k == FCH - 1))
                    pe_out.inc(last)
                assert slot[0] in (0, SLOTS), slot[0]

            passes(pe, body)

        @block.scalar
        def _(act):
            act.sem_inc(act_mm.sem, act_mm.start)
            act.sem_inc(act_tt.sem, act_tt.start)
            act.sem_inc(act_st.sem, act_st.start)
            act.wait_ge(cleared, NCLEAR)

            def copy(dst, src, **kw):
                return nc.scalar.activation(dst, src, ACT.Identity, **kw)

            def body(c, l, it, recur):
                slot = [0]

                def lstm_step():
                    if recur:
                        lstm.on_act(nc, act, step(it, slot[0]))
                        slot[0] += 1

                def take_qk(i, c_):
                    use, n = mm_q(i, c_), 4 * i + c_ + 1
                    pe_mm.wait(act, it, use)
                    qk_in.wait(act, it, n)
                    src = bank(mm, use)
                    nc.scalar.activation(sq[:, c_, :], src[:, :], ACT.Square)
                    act_mm.inc(copy(raw[:, c_, :], src[:, :]))

                def take_v(i, c_):
                    use = mm_q(i, c_)
                    pe_mm.wait(act, it, use)
                    src = bank(mm, use)
                    cols = slice((c_ - 4) * 512, (c_ - 3) * 512)
                    v_in.inc(copy(vb[:, i % 2, cols], src[:, :]))
                    act_mm.inc(copy(va[0:WINDOW, i % 2, cols], src[0:WINDOW, :]))

                def take_turned(i, c_):
                    use = tt_qk(i, c_)
                    pe_tt.wait(act, it, use)
                    src = bank(tt, use)[:, :].rearrange("p (j t) -> p j t", j=4)
                    pairs_ = slice((c_ // 2) * 4, (c_ // 2) * 4 + 4)
                    if c_ % 2 == 0:
                        act_tt.inc(copy(qT[:, pairs_, :], src))
                    else:
                        if c_ == 1 and i % TPC == 1:
                            act.wait_ge(kept_out, it * 64 + 32 * (i // TPC) + 32)
                        if i % TPC == 0:
                            copy(kT[:, 1, pairs_, 2 * WINDOW:3 * WINDOW], src[:, :, WINDOW:2 * WINDOW])
                        act_tt.inc(copy(kT[:, i % 2, pairs_, 0:2 * WINDOW], src))

                def exps(i, g):
                    use = HG * i + g + 1
                    nb_in.wait(act, it, use)
                    src = bank(st, use)
                    for n in range(HG):
                        head, at = head_of(g, n), HG * g + n
                        ins = nc.scalar.activation(pr[:, g % 2, n * TILE:(n + 1) * TILE], src[:, n * TILE:(n + 1) * TILE], ACT.Exp,
                                                   bias=nb[:, at:at + 1], scale=qn[:, i % 2, head:head + 1],
                                                   accum_out=den[:, at:at + 1])
                    act_st.inc(ins)

                def take_p(i, g):
                    use = tt_p(i, g)
                    pe_tt.wait(act, it, use)
                    act_tt.inc(copy(pT[:, g % 2, :], bank(tt, use)[:, :]))

                take_qk(0, 0)
                take_qk(0, 1)
                lstm_step()
                take_qk(0, 2)
                take_qk(0, 3)
                lstm_step()
                take_v(0, 4)
                take_v(0, 5)
                lstm_step()
                take_qk(1, 0)
                take_turned(0, 0)
                take_turned(0, 1)
                for i in range(TPG):
                    more = i + 1 < TPG
                    lstm_step()
                    if i > 0:
                        take_p(i - 1, 3)
                    exps(i, 0)
                    if more:
                        take_qk(i + 1, 1)
                    lstm_step()
                    take_turned(i, 2)
                    take_turned(i, 3)
                    if more:
                        take_qk(i + 1, 2)
                    lstm_step()
                    take_p(i, 0)
                    exps(i, 1)
                    lstm_step()
                    if not more:
                        lstm_step()
                    exps(i, 2)
                    if more:
                        take_qk(i + 1, 3)
                    take_p(i, 1)
                    lstm_step()
                    if more:
                        take_turned(i + 1, 0)
                        take_turned(i + 1, 1)
                        take_v(i + 1, 4)
                    lstm_step()
                    take_p(i, 2)
                    exps(i, 3)
                    if more:
                        take_v(i + 1, 5)
                    lstm_step()
                    if i + 2 < TPG:
                        take_qk(i + 2, 0)
                take_p(TPG - 1, 3)
                for _ in range(5):
                    lstm_step()
                act.wait_ge(vec_in, it + 1)
                for k in range(KT):
                    use = tt_ln(k)
                    pe_tt.wait(act, it, use)
                    act_tt.inc(copy(xnT[:, k, :], bank(tt, use)[:, :], bias=vcol(LNB + k), scale=vcol(LNG + k)))
                for j in range(FCH):
                    use = mm_gate(j)
                    pe_mm.wait(act, it, use)
                    if j >= 2:
                        done(act, dve_dd, it, dd_a(j - 2))
                    act_mm.inc(nc.scalar.activation(gel[0:FW[j], j % 2, :], bank(mm, use)[0:FW[j], :], ACT.Gelu,
                                                    bias=vec[0:FW[j], B1G + j:B1G + j + 1]))
                    if j > 0:
                        lstm_step()
                assert slot[0] in (0, SLOTS), slot[0]

            passes(act, body)

        @block.vector
        def _(dve):
            dve.sem_inc(dve_dd.sem, dve_dd.start)
            dve.sem_inc(qk_in.sem, qk_in.start)
            dve.sem_inc(ffn_out.sem, ffn_out.start)
            dve.sem_inc(out_done, 16)
            dve.wait_ge(cleared, NCLEAR)

            def chunk_start(c):
                dve.wait_ge(lstm.history, (c + 1) * CHUNK)
                for k in range(KT):
                    ins = nc.vector.tensor_copy(tokens(xa, k), lstm.hist[:, bass.ds(c * CHUNK, CHUNK), k * BATCH:(k + 1) * BATCH].rearrange("p t b -> p b t"))
                ins.then_inc(chunk_in, 1)

            def chunk_end(c):
                ffn_out.wait(dve, c * DEPTH + DEPTH, KT)
                dve.wait_ge(xres_in, (c + 1) * 16)
                for k in range(KT):
                    nc.vector.tensor_tensor(by_batch(xres[:, k, :]), tokens(xa, k), by_batch(xres[:, k, :]), ALU.add).then_inc(xres_sum, 1)
                dve.wait_ge(xres_sum, (c + 1) * KT)

            def body(c, l, it, recur):
                slot = [0]

                def lstm_step():
                    if recur:
                        lstm.on_dve(nc, dve, step(it, slot[0]), gates)
                        slot[0] += 1

                def link(ins):
                    chain.wait(dve, it, chain.inc(ins))

                def rotate(i, c_):
                    done(dve, act_mm, it, mm_q(i, c_))
                    tab = rotl[:, i % TPC, 2 * (c_ % 2):2 * (c_ % 2) + 1, :]
                    nc.vector.tensor_tensor(heads(qk[:, c_, :]), heads(raw[:, c_, :]), tab.broadcast_to([P, 8, DHEAD]), ALU.mult)
                    link(nc.vector.tensor_reduce(ss[:, c_, :], heads(sq[:, c_, :]), AX_X, ALU.add))
                    ss_in.inc(nc.vector.tensor_scalar(ss[:, c_, :], ss[:, c_, :], NORM_FLOOR, None, ALU.max))

                def finish(i, c_):
                    n = 4 * i + c_ + 1
                    dst = heads(qk[:, c_, :])
                    hs = slice(8 * (c_ // 2), 8 * (c_ // 2) + 8)
                    turn_in.wait(dve, it, n)
                    ins = nc.vector.tensor_tensor(qk[:, c_, :], qk[:, c_, :], turn[:, c_ % 2, :], ALU.add)
                    if c_ % 2 == 1:
                        link(ins)
                        norm_in.wait(dve, it, n)
                        ins = nc.vector.tensor_tensor(dst, dst, kn[:, hs].rearrange("p (h o) -> p h o", o=1).broadcast_to([P, 8, DHEAD]), ALU.mult)
                    qk_in.inc(ins)

                def maxima(i, g):
                    use = HG * i + g + 1
                    hs = slice(HG * g, HG * g + HG)
                    pe_st.wait(dve, it, use)
                    norm_in.wait(dve, it, 4 * i + 2 * (g // 2) + 1)
                    link(nc.vector.tensor_reduce(mx[:, hs], heads(bank(st, use)[:, :], HG), AX_X, ALU.max))
                    nb_in.inc(nc.vector.scalar_tensor_tensor(nb[:, hs], mx[:, hs], -1.0, qn[:, i % 2, head_of(g, 0):head_of(g, HG - 1) + 1:2], ALU.mult, ALU.mult))

                def normalise(i, g):
                    use = HG * i + g + 1
                    hs = slice(HG * g, HG * g + HG)
                    done(dve, act_st, it, use)
                    link(nc.vector.reciprocal(rden[:, hs], den[:, hs]))
                    dst = heads(pr[:, g % 2, :], HG)
                    pr_in.inc(nc.vector.tensor_tensor(dst, dst, rden[:, hs].rearrange("p (h o) -> p h o", o=1).broadcast_to([P, HG, TILE]), ALU.mult))

                def take_o(i, half):
                    use = dd_o(i, half)
                    pe_dd.wait(dve, it, use)
                    dve_dd.inc(nc.vector.tensor_copy(oT[:, 4 * half:4 * half + 4, i * TILE:(i + 1) * TILE],
                                                     bank(dd, use)[:, :].rearrange("p (j t) -> p j t", j=4)))

                def add_attention(b):
                    for m in range(KT):
                        pe_out.wait(dve, it, KT * b + m + 1)
                        attn_out.inc(nc.vector.tensor_tensor(xb[:, m, b, m:m + CHUNK], mm[m][:, b * CHUNK:(b + 1) * CHUNK], xa[:, m, b, m:m + CHUNK], ALU.add))
                        if b == 0 and m == 0:
                            yield

                def statistics(b):
                    pe_ft.wait(dve, it, b + 1)
                    for i in range(TPC):
                        n = chain.inc(nc.vector.bn_stats(stats[:, TPC * b + i, :], st[b][:, i * DIM:(i + 1) * DIM]))
                    chain.wait(dve, it, n)
                    dve.sem_inc(dve_passed, 1)
                    for i in range(TPC * b, TPC * b + TPC):
                        n = chain.inc(nc.vector.bn_aggr(mv[:, i, :], stats[:, i, :]))
                    chain.wait(dve, it, n)
                    ts = slice(TPC * b, TPC * b + TPC)
                    var_in.inc(nc.vector.tensor_scalar(mv[:, ts, 1], mv[:, ts, 1], LN_EPS, None, ALU.add))

                def standardise(b):
                    rstd_in.wait(dve, it, b + 1)
                    for i in range(TPC):
                        t = TPC * b + i
                        ins = nc.vector.tensor_scalar(xn[:, t, :], st[b][:, i * DIM:(i + 1) * DIM], mv[:, t, 0:1], rstd[:, t:t + 1], ALU.subtract, ALU.mult)
                    xn_in.inc(ins)

                dve.wait_ge(rotl_in, it + 1)
                rotate(0, 0)
                lstm_step()
                rotate(0, 1)
                lstm_step()
                rotate(0, 2)
                finish(0, 0)
                finish(0, 1)
                lstm_step()
                rotate(0, 3)
                finish(0, 2)
                first_add = add_attention(0)
                for i in range(TPG):
                    more = i + 1 < TPG
                    lstm_step()
                    maxima(i, 0)
                    if i == 0:
                        finish(0, 3)
                    if more:
                        rotate(i + 1, 0)
                    lstm_step()
                    normalise(i, 0)
                    if i > 0:
                        take_o(i - 1, 1)
                    if more:
                        rotate(i + 1, 1)
                    lstm_step()
                    maxima(i, 1)
                    if more:
                        finish(i + 1, 0)
                    else:
                        next(first_add)
                    lstm_step()
                    normalise(i, 1)
                    if not more:
                        lstm_step()
                    maxima(i, 2)
                    if more:
                        finish(i + 1, 1)
                        rotate(i + 1, 2)
                    else:
                        next(first_add, None)
                    lstm_step()
                    normalise(i, 2)
                    take_o(i, 0)
                    if more:
                        rotate(i + 1, 3)
                    lstm_step()
                    maxima(i, 3)
                    if more:
                        finish(i + 1, 2)
                    lstm_step()
                    normalise(i, 3)
                    if more:
                        finish(i + 1, 3)
                lstm_step()
                statistics(0)
                take_o(TPG - 1, 1)
                lstm_step()
                standardise(0)
                for _ in add_attention(1):
                    pass
                lstm_step()
                statistics(1)
                lstm_step()
                standardise(1)
                lstm_step()
                dve.wait_ge(vec_in, it + 1)
                attn_out.wait(dve, it, BATCH * KT)
                for j in range(FCH):
                    use = dd_a(j)
                    pe_dd.wait(dve, it, use)
                    done(dve, act_mm, it, mm_gate(j))
                    w = FW[j]
                    dve_dd.inc(nc.vector.scalar_tensor_tensor(u[0:w, j, :], bank(dd, use)[0:w, :], vec[0:w, B1A + j:B1A + j + 1], gel[0:w, j % 2, :],
                                                              ALU.add, ALU.mult))
                    if j > 0:
                        lstm_step()
                for m in range(KT):
                    pe_out.wait(dve, it, BATCH * KT + m + 1)
                    ffn_out.inc(nc.vector.scalar_tensor_tensor(tokens(xa, m), by_batch(mm[m][:, :]), vcol(B2 + m), tokens(xb, m), ALU.add, ALU.add))
                assert slot[0] in (0, SLOTS), slot[0]

            passes(dve, body, chunk_start, chunk_end)
            for n in COUNTS:
                n.check(2)


def rotary_tables(np):
    half = np.arange(0, DHEAD, 2, dtype=np.float32)
    inv_freq = (1.0 / np.float32(10000.0) ** (half / np.float32(DHEAD))).astype(np.float32)
    t = np.arange(SEQ, dtype=np.float32)
    freqs = t[:, None] * inv_freq[None, :]
    freqs = np.concatenate([freqs, freqs], -1)
    base = (half + np.float32(0.4 * DHEAD)) / np.float32(1.4 * DHEAD)
    power = (t - SEQ // 2) / np.float32(WINDOW // 2)
    scale = (base[None, :] ** power[:, None]).astype(np.float32)
    scale = np.concatenate([scale, scale], -1)
    sign = np.concatenate([-np.ones(DHEAD // 2), np.ones(DHEAD // 2)]).astype(np.float32)
    cos, sin = np.cos(freqs), np.sin(freqs) * sign
    return np.stack([QK_SCALE * cos * scale, QK_SCALE * sin * scale, cos / scale, sin / scale], 1).astype(np.float32)


def window_masks(np):
    i, j = np.arange(WINDOW)[:, None], np.arange(WINDOW)[None, :]
    own, before = np.where(j <= i, 0.0, MASKED), np.where(j >= i, 0.0, MASKED)
    none = np.full((WINDOW, WINDOW), MASKED)
    second = np.concatenate([before, own], 1)
    return np.stack([np.concatenate([np.concatenate([own, b], 1), second], 0) for b in (none,) + (before,) * (CHUNKS - 1)])


def kernel(x, cond_1024, L0_cond_Wx, L0_cond_Wh, L0_cond_b, L0_ffn_Wqkv, L0_ffn_q_scale, L0_ffn_k_scale, L0_ffn_Wo,
           L0_ffn_ln_g, L0_ffn_ln_b, L0_ffn_W1, L0_ffn_b1, L0_ffn_W2, L0_ffn_b2):
    import ml_dtypes
    import numpy as np
    import concourse.bacc as bacc
    from concourse.bass_utils import run_bass_kernel_spmd

    def rows(w):
        w = np.asarray(w)
        pad = -w.shape[-2] % P
        w = np.concatenate([w, np.zeros((*w.shape[:-2], pad, w.shape[-1]), w.dtype)], -2)
        return np.swapaxes(w.reshape(*w.shape[:-2], -1, P, w.shape[-1]), -3, -2)

    def flat(w):
        return w.reshape(*w.shape[:-2], -1)

    def cols(v):
        return rows(np.asarray(v)[..., None])[..., 0]

    b1 = np.asarray(L0_ffn_b1)
    vecs = np.concatenate([cols(v) for v in (b1[:, :FF], b1[:, FF:], L0_ffn_ln_g, L0_ffn_ln_b, L0_ffn_b2)], -1)
    q_scale, k_scale = np.asarray(L0_ffn_q_scale), np.asarray(L0_ffn_k_scale)
    swap = lambda v: np.roll(v, DHEAD // 2, -1)
    xh = np.asarray(x)
    nc = bacc.Bacc("TRN2", target_bir_lowering=False, num_devices=1)
    given = {
        "x_cols": rows(xh.transpose(2, 0, 1).reshape(DIM, BATCH * SEQ)),
        "h0_cols": flat(rows(np.asarray(cond_1024).T)),
        "Wx": rows(L0_cond_Wx), "Wh": rows(L0_cond_Wh), "b_cols": cols(L0_cond_b),
        "Wqkv": flat(rows(L0_ffn_Wqkv)), "qk_scales": np.concatenate([q_scale, swap(q_scale), k_scale, swap(k_scale)], -1),
        "Wo": flat(rows(L0_ffn_Wo)), "W1": flat(rows(L0_ffn_W1)), "W2": flat(rows(L0_ffn_W2)),
        "layer_vecs": np.swapaxes(vecs, 0, 1),
        "rotary": rotary_tables(np), "masks": window_masks(np).astype(ml_dtypes.bfloat16), "identity": np.eye(P, dtype=np.float32),
    }
    arrays = {f"in_{n}": np.ascontiguousarray(a) for n, a in given.items()}
    args = [nc.dram_tensor(n, a.shape, mybir.dt.from_np(a.dtype), kind="ExternalInput").ap() for n, a in arrays.items()]
    args.append(nc.dram_tensor("out_cols", (P, KT, BATCH * SEQ), F32, kind="ExternalOutput").ap())
    build_program(nc, *args)
    r = run_bass_kernel_spmd(nc, [arrays], core_ids=[0])
    got = np.asarray(r.results[0]["out_cols"])
    return np.ascontiguousarray(got.transpose(1, 0, 2).reshape(DIM, BATCH, SEQ).transpose(1, 2, 0))
```

```python
from contextlib import ExitStack

import concourse.bass as bass
from concourse import mybir

F32 = mybir.dt.float32
BF16 = mybir.dt.bfloat16
ALU = mybir.AluOpType
ACT = mybir.ActivationFunctionType
AX_X = mybir.AxisListType.X

P = 128
BATCH, SEQ, DIM = 2, 1024, 256
KT = DIM // P
DEPTH, HEADS, DHEAD, WINDOW = 6, 16, 64, 64
INNER = HEADS * DHEAD
FF = int(DIM * 4 * 2 / 3)
FCH = (FF + P - 1) // P
FW = [min(P, FF - P * j) for j in range(FCH)]
GATES = 4 * DIM
GM = GATES // P
QK_SCALE = 8.0
LN_EPS = 1e-5
NORM_FLOOR = 1e-24
MASKED = -1.0e30

TILE = 128
CHUNK = 256
CHUNKS = SEQ // CHUNK
GROUP = BATCH * CHUNK
TPG = GROUP // TILE
TPC = CHUNK // TILE
ROW = CHUNK + 1
PARTS = 3
HC = KT * BATCH
XWC = GM * PARTS * BATCH
UNROLL = 4
SLOTS = 42
HALFS = SLOTS // 2
LEAD = SEQ - (CHUNKS - 1) * DEPTH * SLOTS
assert LEAD >= CHUNK and LEAD % UNROLL == 0 and all(LEAD + c * DEPTH * SLOTS >= (c + 1) * CHUNK for c in range(CHUNKS))
CHAIN = TPG * (2 * 1 + 2 * 2 + 4 + 4 + 2)


class Count:

    def __init__(self, sem, per, start=0):
        self.sem, self.per, self.start, self.n = sem, per, start, 0

    def inc(self, ins):
        self.n += 1
        ins.then_inc(self.sem, 1)
        return (self.n - 1) % self.per + 1

    def check(self, passes):
        assert self.n == self.per * passes, (self.sem, self.n, self.per)

    def wait(self, eng, it, n):
        eng.wait_ge(self.sem, it * self.per + n)


def pairs(ap):
    return ap.rearrange("p (a b) -> p a b", b=BATCH)


class Lstm:

    OC = KT * PARTS * BATCH
    LATER = [*range(KT, GM), *range(KT)]

    def __init__(self, sb, sem):
        self.whp = sb("whp", [P, PARTS, KT, GATES], BF16)
        self.state = sb("state", [P, 5 * HC])
        self.uv = sb("uv", [P, 2 * HC])
        self.tcell = sb("tcell", [P, HC])
        self.gsum = sb("gsum", [P, GM * BATCH])
        self.h32 = sb("h32", [P, HC])
        self.hrest = sb("hrest", [P, HC])
        self.hp = sb("hp", [P, KT, PARTS, BATCH], BF16)
        self.hist = sb("hist", [P, SEQ, HC])
        self.gates_done, self.gates_summed, self.gates_act = sem("gates_done"), sem("gates_summed"), sem("gates_act")
        self.out_done, self.out_summed, self.out_act = sem("out_done"), sem("out_summed"), sem("out_act")
        self.uv_done, self.cell_done, self.cell_tanh = sem("uv_done"), sem("cell_done"), sem("cell_tanh")
        self.h_hi, self.h_chain, self.h_rest, self.h_parts = sem("h_hi"), sem("h_chain"), sem("h_rest"), sem("h_parts")
        self.history = sem("history")

    def on_pe(self, nc, pe, t, g, go, ident16, xw_t):
        oc = self.OC
        if g is go:
            pe.wait_ge(self.gates_summed, t)
            nc.tensor.matmul(g[:, 0:XWC], ident16[:, :], xw_t, start=True, stop=False, skip_group_check=True)
        else:
            pe.wait_ge(self.out_summed, t + 1)
            nc.tensor.matmul(g[:, oc:XWC], ident16[:, :], xw_t[:, oc:XWC], start=True, stop=False, skip_group_check=True)
            nc.tensor.matmul(go[:, 0:oc], ident16[:, :], xw_t[:, 0:oc], start=True, stop=False, skip_group_check=True)
        pe.wait_ge(self.h_hi, t + 1)
        for m in self.LATER:
            bk = go if m < KT else g
            for k in range(KT):
                nc.tensor.matmul(bk[:, m * PARTS * BATCH:m * PARTS * BATCH + BATCH], self.whp[:, 2, k, m * P:(m + 1) * P],
                                 self.hp[:, k, 0, :], start=False, stop=False, skip_group_check=True)
        pe.wait_ge(self.h_parts, t + 1)
        for m in self.LATER:
            bk = go if m < KT else g
            for p in (1, 0):
                for k in range(KT):
                    last = nc.tensor.matmul(bk[:, m * PARTS * BATCH:(m + 1) * PARTS * BATCH], self.whp[:, p, k, m * P:(m + 1) * P],
                                            self.hp[:, k, :, :].rearrange("p a b -> p (a b)"), start=False, stop=(m in (GM - 1, KT - 1)),
                                            skip_group_check=True)
            if m == GM - 1:
                last.then_inc(self.gates_done, 1)
        last.then_inc(self.out_done, 1)

    def on_act(self, nc, act, t, apart):
        act.wait_ge(self.gates_summed, t + 1)
        if apart:
            nc.scalar.activation(self.state[:, HC:4 * HC], self.gsum[:, HC:4 * HC], ACT.Tanh).then_inc(self.gates_act, 1)
            act.wait_ge(self.out_summed, t + 3)
            nc.scalar.activation(self.state[:, 0:HC], self.gsum[:, 0:HC], ACT.Tanh).then_inc(self.out_act, 1)
        else:
            nc.scalar.activation(self.state[:, 0:4 * HC], self.gsum[:, 0:4 * HC], ACT.Tanh).then_inc(self.gates_act, 1)
        act.wait_ge(self.cell_done, t + 1)
        nc.scalar.activation(self.tcell[:, :], self.state[:, 4 * HC:5 * HC], ACT.Tanh, scale=0.5).then_inc(self.cell_tanh, 1)

    def on_dve(self, nc, dve, t, g, go):
        state, uv, hp, h32, oc = self.state, self.uv, self.hp, self.h32, self.OC

        def gate_sums(bk, lo, hi):
            return nc.vector.tensor_reduce(self.gsum[:, lo * BATCH:hi * BATCH].rearrange("p (m b) -> p m b", b=BATCH),
                                           bk[:, lo * PARTS * BATCH:hi * PARTS * BATCH].rearrange("p (m q b) -> p m b q", q=PARTS, b=BATCH), AX_X, ALU.add)

        if g is go:
            dve.wait_ge(self.out_done, t + 1)
            gate_sums(g, 0, GM).then_inc(self.gates_summed, 1)
            dve.wait_ge(self.gates_act, t + 1)
        else:
            dve.wait_ge(self.gates_done, t + 1)
            gate_sums(g, KT, GM).then_inc(self.gates_summed, 1)
            dve.wait_ge(self.out_done, t + 1)
            gate_sums(go, 0, KT).then_inc(self.out_summed, 1)
            dve.wait_ge(self.gates_act, t + 1)
        nc.vector.scalar_tensor_tensor(uv[:, :], state[:, HC:3 * HC], 1.0, state[:, 3 * HC:5 * HC], ALU.add, ALU.mult).then_inc(self.uv_done, 1)
        dve.wait_ge(self.uv_done, t + 1)
        nc.vector.scalar_tensor_tensor(state[:, 4 * HC:5 * HC], uv[:, HC:2 * HC], 0.5, uv[:, 0:HC], ALU.mult, ALU.add).then_inc(self.cell_done, 1)
        if g is not go:
            dve.wait_ge(self.out_act, t + 1)
        dve.wait_ge(self.cell_tanh, t + 1)
        nc.vector.scalar_tensor_tensor(hp[:, :, 0, :], pairs(state[:, 0:HC]), 1.0, pairs(self.tcell[:, :]), ALU.add, ALU.mult).then_inc(self.h_hi, 1)
        nc.vector.scalar_tensor_tensor(h32[:, :], state[:, 0:HC], 1.0, self.tcell[:, :], ALU.add, ALU.mult).then_inc(self.h_chain, 1)
        dve.wait_ge(self.h_hi, t + 2)
        dve.wait_ge(self.h_chain, 2 * t + 1)
        nc.vector.tensor_tensor(hp[:, :, 1, :], pairs(h32[:, :]), hp[:, :, 0, :], ALU.subtract).then_inc(self.h_chain, 1)
        nc.vector.tensor_tensor(pairs(self.hrest[:, :]), pairs(h32[:, :]), hp[:, :, 0, :], ALU.subtract).then_inc(self.h_rest, 1)
        dve.wait_ge(self.h_chain, 2 * t + 2)
        dve.wait_ge(self.h_rest, t + 1)
        nc.vector.tensor_tensor(hp[:, :, 2, :], pairs(self.hrest[:, :]), hp[:, :, 1, :], ALU.subtract).then_inc(self.h_parts, 1)
        nc.vector.tensor_scalar(self.hist[:, bass.ds(t, 1), :].rearrange("p a n -> p (a n)"), h32[:, :], 0.5, None, ALU.mult).then_inc(self.history, 1)


def build_program(nc, x_cols, h0_cols, Wx, Wh, b_cols, Wqkv, qk_scales, Wo, W1, W2, layer_vecs, rotary, masks, identity, out):
    with ExitStack() as ctx:
        def sb(name, shape, dt=F32, c=ctx):
            return c.enter_context(nc.sbuf_tensor(name, shape, dt))

        def sem(name, c=ctx):
            return c.enter_context(nc.semaphore(name))

        ident = sb("ident", [P, P])
        ident16 = sb("ident16", [P, P], BF16)
        vecs = sb("vecs", [P, DEPTH, 2 * FCH + 3 * KT])
        wqkv = sb("wqkv", [P, KT * 3 * INNER])
        wo = sb("wo", [P, INNER // P * DIM])
        w1 = sb("w1", [P, KT * 2 * FF])
        w2 = sb("w2", [P, FCH * DIM])
        weights = [(w, src, sem(f"w_in{n}")) for n, (w, src) in enumerate(((wqkv, Wqkv), (wo, Wo), (w1, W1), (w2, W2)))]
        lstm = Lstm(sb, sem)
        xw_dram = nc.dram_tensor("xw_parts", (P, (SEQ + SLOTS) * XWC), BF16, kind="Internal").ap()
        k_dram = nc.dram_tensor("k_windows", (DEPTH, BATCH, P, HEADS // 2 * WINDOW), F32, kind="Internal").ap()
        v_dram = nc.dram_tensor("v_windows", (DEPTH, BATCH, WINDOW, INNER), F32, kind="Internal").ap()
        lstm_stage(nc, sb, sem, lstm, x_cols, h0_cols, Wx, Wh, b_cols, layer_vecs, identity, ident, ident16, vecs, weights,
                   xw_dram, k_dram, v_dram)
        layer_stage(nc, sb, sem, lstm, x_cols, qk_scales, rotary, masks, ident, ident16, vecs, weights, xw_dram, k_dram, v_dram, out)


def lstm_stage(nc, sb0, sem0, lstm, x_cols, h0_cols, Wx, Wh, b_cols, layer_vecs, identity, ident, ident16, vecs, weights,
               xw_dram, k_dram, v_dram):
    with ExitStack() as ctx:
        def sb(name, shape, dt=F32):
            return sb0(name, shape, dt, ctx)

        def sem(name):
            return sem0(name, ctx)

        xw = sb("xw", [P, SEQ, XWC], BF16)
        wh32 = sb("wh32", [P, KT, GATES])
        wx_sb = sb("wx_sb", [P, KT, GATES])
        xT = sb("xT", [P, KT, BATCH * SEQ])
        bias = sb("bias", [P, GM])
        scratch = lstm.hist[:, :, :].rearrange("p t n -> p (t n)")
        zero = scratch[:, SEQ * HC - INNER:SEQ * HC]
        rest32 = scratch[:, SEQ * HC - INNER - 512:SEQ * HC - INNER]
        part32 = scratch[:, SEQ * HC - INNER - 1536:SEQ * HC - INNER - 512].rearrange("p (a n) -> p a n", a=2)
        assert LEAD * HC <= SEQ * HC - INNER - 1536
        rest_pool = wh32[:, 0, 0:512]
        whp, hp, h32, hrest = lstm.whp, lstm.hp, lstm.h32, lstm.hrest
        ps = [ctx.enter_context(nc.psum_tensor(f"gates{i}", [P, 512], F32)) for i in range(2)]
        pj = [ctx.enter_context(nc.psum_tensor(f"proj{i}", [P, 512], F32)) for i in range(2)]
        po = [ctx.enter_context(nc.psum_tensor(f"out_gate{i}", [P, 512], F32)) for i in range(2)]

        const_in, wx_in, wh_in, h0_in, xt_in = sem("const_in"), sem("wx_in"), sem("wh_in"), sem("h0_in"), sem("xt_in")
        zeroed, bias_ready, h_ready, spilled = sem("zeroed"), sem("bias_ready"), sem("h_ready"), sem("spilled")
        wh_chain, wh_split, late_split, late_chain = sem("wh_chain"), sem("wh_split"), sem("late_split"), sem("late_chain")
        projected, xw_evac, xw_split, xw_chain = sem("projected"), sem("xw_evac"), sem("xw_split"), sem("xw_chain")
        NE = GM * BATCH
        EARLY = [(m, b, 0) for m in range(GM) for b in range(BATCH)]
        LATE = [(m, b, t0) for t0 in range(512, SEQ, 512) for m in range(GM) for b in range(BATCH)]
        PIECES = EARLY + LATE
        STEPS_PER_PIECE = 3
        SPREAD = STEPS_PER_PIECE * len(LATE)
        assert STEPS_PER_PIECE > KT and LEAD <= 512 and SPREAD <= LEAD and SPREAD % 2 == 0 and (LEAD - SPREAD) % UNROLL == 0

        def parts_of(n):
            m, b, t0 = PIECES[n]
            return [xw[:, t0:t0 + 512, (m * PARTS + q) * BATCH + b] for q in range(PARTS)]

        def steps(eng, one_step, between):
            for t in range(SPREAD):
                one_step(t, t % 2)
                between(NE + t // STEPS_PER_PIECE, t % STEPS_PER_PIECE)
            with eng.Fori(0, (LEAD - SPREAD) // UNROLL) as it:
                for u in range(UNROLL):
                    one_step(it * UNROLL + (SPREAD + u), u % 2)

        block = ctx.enter_context(nc.Block("lstm"))

        @block.sync
        def _(sp):
            sp.dma_start(wx_sb[:, :, :], Wx).then_inc(wx_in, 16)
            sp.dma_start(xT[:, :, :], x_cols).then_inc(xt_in, 16)
            sp.dma_start(bias[:, :], b_cols).then_inc(h0_in, 16)
            sp.dma_start(h32[:, :], h0_cols).then_inc(h0_in, 16)
            sp.dma_start(ident[:, :], identity).then_inc(const_in, 16)
            sp.dma_start(vecs[:, :, :], layer_vecs).then_inc(const_in, 16)
            sp.dma_start(wh32[:, :, :], Wh).then_inc(wh_in, 16)
            for w, src, landed in weights:
                sp.dma_start(w[:, :], src[0, :, :]).then_inc(landed, 16)
            sp.wait_ge(zeroed, 2)
            for l in range(DEPTH):
                for bt in range(BATCH):
                    sp.dma_start(k_dram[l, bt, :, :], zero[:, 0:HEADS // 2 * WINDOW]).then_inc(spilled, 16)
                    sp.dma_start(v_dram[l, bt, :, :], zero[0:WINDOW, :]).then_inc(spilled, 16)
            sp.wait_ge(xw_split, NE)
            sp.wait_ge(late_split, len(LATE))
            sp.dma_start(xw_dram[:, LEAD * XWC:SEQ * XWC], xw[:, LEAD:SEQ, :].rearrange("p t n -> p (t n)")).then_inc(spilled, 16)
            sp.dma_start(xw_dram[:, SEQ * XWC:(SEQ + SLOTS) * XWC], xw[:, 0:SLOTS, :].rearrange("p t n -> p (t n)")).then_inc(spilled, 16)
            sp.wait_ge(spilled, 16 * (2 * DEPTH * BATCH + 2))

        @block.gpsimd
        def _(pool):
            nc.gpsimd.memset(lstm.state[:, :], 0.0).then_inc(zeroed, 1)
            nc.gpsimd.memset(zero, 0.0).then_inc(zeroed, 1)
            n_wh, n_late = [0], [0]

            def link(ins, n, chain):
                n[0] += 1
                ins.then_inc(chain, 1)
                pool.wait_ge(chain, n[0])

            pool.wait_ge(wh_in, 16)
            for k in range(KT):
                for c in range(GATES // 512):
                    cols = slice(c * 512, (c + 1) * 512)
                    w = wh32[:, k, cols]
                    for half in range(2):
                        hw = w[:, half * DIM:(half + 1) * DIM]
                        link(nc.gpsimd.tensor_scalar(hw, hw, 0.5 if 2 * c + half == 3 else 0.25, None, ALU.mult), n_wh, wh_chain)
                    link(nc.gpsimd.tensor_copy(whp[:, 0, k, cols], w), n_wh, wh_chain)
                    link(nc.gpsimd.tensor_tensor(w, w, whp[:, 0, k, cols], ALU.subtract), n_wh, wh_chain)
                    link(nc.gpsimd.tensor_copy(whp[:, 1, k, cols], w), n_wh, wh_chain)
                    link(nc.gpsimd.tensor_tensor(whp[:, 2, k, cols], w, whp[:, 1, k, cols], ALU.subtract), n_wh, wh_chain)
            pool.sem_inc(wh_split, 1)
            for n in range(NE, len(PIECES)):
                pool.wait_ge(xw_evac, n + 1)
                src, at = part32[:, n % 2, :], parts_of(n)
                link(nc.gpsimd.tensor_copy(at[0], src), n_late, late_chain)
                link(nc.gpsimd.tensor_tensor(rest_pool, src, at[0], ALU.subtract), n_late, late_chain)
                link(nc.gpsimd.tensor_copy(at[1], rest_pool), n_late, late_chain)
                nc.gpsimd.tensor_tensor(at[2], rest_pool, at[1], ALU.subtract).then_inc(late_split, 1)
                pool.wait_ge(late_split, n - NE + 1)

        @block.tensor
        def _(pe):
            pe.wait_ge(xt_in, 16)
            pe.wait_ge(wx_in, 16)

            def piece(n, k):
                m, b, t0 = PIECES[n]
                if n >= 2 and k == 0:
                    pe.wait_ge(xw_evac, n - 1)
                ins = nc.tensor.matmul(pj[n % 2][:, :], wx_sb[:, k, m * P:(m + 1) * P], xT[:, k, b * SEQ + t0:b * SEQ + t0 + 512],
                                       start=(k == 0), stop=(k == KT - 1))
                if k == KT - 1:
                    ins.then_inc(projected, 1)

            for n in range(NE):
                for k in range(KT):
                    piece(n, k)
            pe.wait_ge(xw_split, NE)
            pe.wait_ge(wh_split, 1)
            pe.wait_ge(h_ready, 1)
            steps(pe, lambda t, u: lstm.on_pe(nc, pe, t, ps[u], po[u], ident16, xw[:, t, :]), lambda n, phase: piece(n, phase) if phase < KT else None)

        @block.scalar
        def _(act):
            act.wait_ge(bias_ready, 1)

            def piece(n):
                m = PIECES[n][0]
                act.wait_ge(projected, n + 1)
                if n >= NE + 2:
                    act.wait_ge(late_split, n - NE - 1)
                elif n >= 2:
                    act.wait_ge(xw_split, n - 1)
                nc.scalar.activation(part32[:, n % 2, :], pj[n % 2][:, :], ACT.Identity, bias=bias[:, m:m + 1],
                                     scale=1.0 if m // KT == 3 else 0.5).then_inc(xw_evac, 1)

            for n in range(NE):
                piece(n)
            steps(act, lambda t, u: lstm.on_act(nc, act, t, True), lambda n, phase: piece(n) if phase == KT else None)

        @block.vector
        def _(dve):
            n_chain = [0]

            def link(ins):
                n_chain[0] += 1
                ins.then_inc(xw_chain, 1)
                dve.wait_ge(xw_chain, n_chain[0])

            dve.wait_ge(h0_in, 32)
            nc.vector.tensor_scalar(bias[:, 0:3 * KT], bias[:, 0:3 * KT], 0.5, None, ALU.mult).then_inc(bias_ready, 1)
            dve.wait_ge(const_in, 32)
            link(nc.vector.tensor_copy(ident16[:, :], ident[:, :]))
            link(nc.vector.tensor_scalar(h32[:, :], h32[:, :], 2.0, None, ALU.mult))
            link(nc.vector.tensor_copy(hp[:, :, 0, :], pairs(h32[:, :])))
            link(nc.vector.tensor_tensor(pairs(hrest[:, :]), pairs(h32[:, :]), hp[:, :, 0, :], ALU.subtract))
            link(nc.vector.tensor_copy(hp[:, :, 1, :], pairs(hrest[:, :])))
            link(nc.vector.tensor_tensor(hp[:, :, 2, :], pairs(hrest[:, :]), hp[:, :, 1, :], ALU.subtract))
            for n in range(NE):
                dve.wait_ge(xw_evac, n + 1)
                src, at = part32[:, n % 2, :], parts_of(n)
                link(nc.vector.tensor_copy(at[0], src))
                link(nc.vector.tensor_tensor(rest32, src, at[0], ALU.subtract))
                link(nc.vector.tensor_copy(at[1], rest32))
                nc.vector.tensor_tensor(at[2], rest32, at[1], ALU.subtract).then_inc(xw_split, 1)
                dve.wait_ge(xw_split, n + 1)
            dve.wait_ge(zeroed, 2)
            dve.sem_inc(lstm.out_summed, 2)
            dve.sem_inc(lstm.h_hi, 1)
            dve.sem_inc(lstm.h_parts, 1)
            dve.sem_inc(h_ready, 1)
            steps(dve, lambda t, u: lstm.on_dve(nc, dve, t, ps[u], po[u]), lambda n, phase: None)


def layer_stage(nc, sb0, sem0, lstm, x_cols, qk_scales, rotary, masks, ident, ident16, vecs, weights, xw_dram, k_dram, v_dram, out):
    with ExitStack() as ctx:
        def sb(name, shape, dt=F32):
            return sb0(name, shape, dt, ctx)

        def sem(name):
            return sem0(name, ctx)

        HALF = DHEAD // 2
        HG = 4
        (wqkv_, wqkv_src, wqkv_in), (wo_, wo_src, wo_in), (w1_, w1_src, w1_in), (w2_, w2_src, w2_in) = weights
        wqkv = wqkv_[:, :].rearrange("p (k n) -> p k n", k=KT)
        wo = wo_[:, :].rearrange("p (k n) -> p k n", n=DIM)
        w1 = w1_[:, :].rearrange("p (k n) -> p k n", k=KT)
        w2 = w2_[:, :].rearrange("p (k n) -> p k n", n=DIM)
        xa = sb("xa", [P, KT, BATCH, ROW])
        xb = sb("xb", [P, KT, BATCH, ROW])
        edge_a = sb("edge_a", [P, DEPTH, BATCH])
        edge_b = sb("edge_b", [P, DEPTH, BATCH])
        xres = sb("xres", [P, KT, GROUP])
        xwp = sb("xwp", [P, SLOTS, XWC], BF16)
        rot = sb("rot", [P, CHUNKS * TPC, 4 * DHEAD])
        rotl = sb("rotl", [P, TPC, 4, DHEAD])
        scales = sb("scales", [P, 4 * DHEAD])
        mask = sb("mask", [P, CHUNKS, TILE], BF16)
        vec = sb("vec", [P, 2 * FCH + 3 * KT])
        raw = sb("raw", [P, 4, 512])
        sq = sb("sq", [P, 4, 512])
        qk = sb("qk", [P, 4, 512])
        turn = sb("turn", [P, 2, 512])
        ss = sb("ss", [P, 4, 8])
        qn = sb("qn", [P, 2, HEADS])
        kn = sb("kn", [P, HEADS])
        power = sb("power", [P, 8])
        va = sb("va", [P, 2, INNER])
        vb = sb("vb", [P, 2, INNER])
        qT = sb("qT", [P, HEADS // 2, TILE])
        kT = sb("kT", [P, 2, HEADS // 2, 3 * WINDOW])
        mx = sb("mx", [P, HEADS])
        nb = sb("nb", [P, HEADS])
        den = sb("den", [P, HEADS])
        rden = sb("rden", [P, HEADS])
        u = sb("u", [P, FCH, GROUP])
        pr, pT = u[:, 0:2, :], u[:, 2:4, :]
        oT = sb("oT", [P, INNER // P, GROUP])
        stats = sb("stats", [P, TPG, 6])
        mv = sb("mv", [P, TPG, 2])
        rstd = sb("rstd", [P, TPG])
        xn = sb("xn", [P, TPG, DIM])
        xnT = sb("xnT", [P, KT, GROUP])
        gel = sb("gel", [P, 2, GROUP])

        def pb(name):
            return ctx.enter_context(nc.psum_tensor(name, [P, 512], F32))

        mm = [pb("mm0"), pb("mm1")]
        dd = [pb("dd")]
        tt = [pb("tt0"), pb("tt1")]
        st = [pb("st0"), pb("st1")]
        gates = pb("gates")

        sc_in, cst_in, cleared = sem("scales_in"), sem("cst_in"), sem("cleared")
        xres_in, xres_sum, stored = sem("xres_in"), sem("xres_sum"), sem("stored")
        xw_in = [sem("xw_in0"), sem("xw_in1")]
        kept_in, kept_out = sem("kept_in"), sem("kept_out")
        chunk_in, rotl_in, vec_in = sem("chunk_in"), sem("rotl_in"), sem("vec_in")
        pool_passed, dve_passed, sp_passed = sem("pool_passed"), sem("dve_passed"), sem("sp_passed")

        pe_mm = Count(sem("pe_mm"), 6 * TPG + FCH)
        act_mm = Count(sem("act_mm"), 6 * TPG + FCH, 2)
        pe_dd = Count(sem("pe_dd"), 2 * TPG + FCH)
        dve_dd = Count(sem("dve_dd"), 2 * TPG + FCH, 1)
        pe_tt = Count(sem("pe_tt"), 8 * TPG + BATCH * KT)
        act_tt = Count(sem("act_tt"), 8 * TPG + BATCH * KT, 2)
        pe_st = Count(sem("pe_st"), HG * TPG)
        act_st = Count(sem("act_st"), HG * TPG, 2)
        pe_out = Count(sem("pe_out"), BATCH * KT + KT)
        ss_in = Count(sem("ss_in"), 4 * TPG)
        norm_in = Count(sem("norm_in"), 4 * TPG)
        var_in = Count(sem("var_in"), BATCH)
        rstd_in = Count(sem("rstd_in"), BATCH)
        pe_ft = Count(sem("pe_ft"), BATCH)
        xn_in = Count(sem("xn_in"), BATCH)
        turn_in = Count(sem("turn_in"), 4 * TPG)
        qk_in = Count(sem("qk_in"), 4 * TPG, 4)
        nb_in = Count(sem("nb_in"), HG * TPG)
        pr_in = Count(sem("pr_in"), HG * TPG)
        v_in = Count(sem("v_in"), 2 * TPG)
        vup_in = Count(sem("vup_in"), 2)
        chain = Count(sem("dve_chain"), CHAIN)
        edge_a_in = Count(sem("edge_a_in"), 2)
        edge_b_in = Count(sem("edge_b_in"), 2)
        attn_out = Count(sem("attn_out"), BATCH * KT)
        ffn_out = Count(sem("ffn_out"), KT, KT)

        def mm_q(i, c): return 6 * i + c + 1
        def mm_gate(j): return 6 * TPG + j + 1
        def dd_o(i, half): return 2 * i + half + 1
        def dd_a(j): return 2 * TPG + j + 1
        TURNS = [("qk", 0, 0), ("qk", 0, 1)]
        for i in range(TPG):
            TURNS += [("p", i - 1, 3)] * (i > 0) + [("qk", i, 2), ("qk", i, 3), ("p", i, 0), ("p", i, 1)]
            TURNS += [("qk", i + 1, 0), ("qk", i + 1, 1)] * (i + 1 < TPG) + [("p", i, 2)]
        TURNS += [("p", TPG - 1, 3)]
        def tt_qk(i, c): return TURNS.index(("qk", i, c)) + 1
        def tt_p(i, g): return TURNS.index(("p", i, g)) + 1
        def tt_ln(b, k): return 8 * TPG + KT * b + k + 1

        def bank(banks, use): return banks[(use - 1) % len(banks)]

        def freed(eng, sem_, it, use):
            sem_.wait(eng, it, use)

        def done(eng, sem_, it, use):
            sem_.wait(eng, it, use + sem_.start)

        def head_of(g, n):
            return 8 * (g // 2) + g % 2 + 2 * n

        def vcol(j, n=1): return vec[:, j:j + n]
        B1A, B1G, LNG, LNB, B2 = 0, FCH, 2 * FCH, 2 * FCH + KT, 2 * FCH + 2 * KT

        def heads(ap, n=8): return ap.rearrange("p (h d) -> p h d", h=n)

        def columns(buf, i, k, shifted):
            c0 = (i % TPC) * TILE + (0 if shifted else k)
            return buf[:, k, i // TPC, c0:c0 + TILE]

        def tokens(buf, m):
            return buf[:, m, :, m:m + CHUNK]

        def by_batch(ap): return ap.rearrange("p (b t) -> p b t", b=BATCH)

        def step(it, slot): return it * SLOTS + (LEAD + slot)

        def passes(eng, body, chunk_start=None, chunk_end=None):
            with eng.Fori(0, CHUNKS - 1) as c:
                if chunk_start:
                    chunk_start(c)
                with eng.Fori(0, DEPTH) as l:
                    body(c, l, c * DEPTH + l, True)
                if chunk_end:
                    chunk_end(c)
            c = CHUNKS - 1
            if chunk_start:
                chunk_start(c)
            with eng.Fori(0, DEPTH) as l:
                body(c, l, l + c * DEPTH, False)
            if chunk_end:
                chunk_end(c)

        DENSE = (1, 4)
        NCLEAR = 5
        COUNTS = [v for v in locals().values() if isinstance(v, Count)]

        block = ctx.enter_context(nc.Block("layers"))

        @block.sync
        def _(sp):
            def passed():
                sp.sem_inc(sp_passed, 1)

            def load_kept(l, bt):
                passed()
                sp.dma_start(kT[:, 0, :, 2 * WINDOW:3 * WINDOW],
                             k_dram[bass.ds(l, 1), bt, :, :].rearrange("a p (j t) -> p (a j) t", t=WINDOW)).then_inc(kept_in, 16)
                sp.dma_start(va[WINDOW:P, 0, :], v_dram[bass.ds(l, 1), bt, :, :].rearrange("a p n -> (a p) n")).then_inc(kept_in, 16)

            def store_kept(l, bt):
                passed()
                sp.dma_start(k_dram[bass.ds(l, 1), bt, :, :].rearrange("a p (j t) -> p (a j) t", t=WINDOW),
                             kT[:, 1, :, WINDOW:2 * WINDOW]).then_inc(kept_out, 16)
                sp.dma_start(v_dram[bass.ds(l, 1), bt, :, :].rearrange("a p n -> (a p) n"), vb[WINDOW:P, 1, :]).then_inc(kept_out, 16)

            def load_weight(n, l):
                passed()
                w, src, landed = weights[n]
                sp.dma_start(w[:, :], src[bass.ds(l, 1), :, :].rearrange("a p n -> (a p) n")).then_inc(landed, 16)

            def load_scales(l):
                passed()
                sp.dma_start(scales[:, :], qk_scales[bass.ds(l, 1), :].partition_broadcast(P).rearrange("p a n -> p (a n)")).then_inc(sc_in, 16)

            def load_xw(n, step0):
                passed()
                sp.dma_start(xwp[:, n * HALFS:(n + 1) * HALFS, :].rearrange("p t n -> p (t n)"),
                             xw_dram[:, bass.ds(step0 * XWC, HALFS * XWC)]).then_inc(xw_in[n], 16)

            def body(c, l, it, recur, nxt):
                sp.wait_ge(kept_out, it * 64 + 32)
                passed()
                pe_dd.wait(sp, it, dd_o(0, 1))
                load_kept(l, 1)
                done(sp, act_tt, it, tt_qk(1, 3))
                passed()
                v_in.wait(sp, it, 4)
                store_kept(l, 0)
                sp.wait_ge(rotl_in, it + 1)
                load_scales(nxt)
                pe_mm.wait(sp, it, mm_q(TPG - 1, 5))
                load_weight(0, nxt)
                pe_dd.wait(sp, it, dd_o(2, 1))
                load_kept(nxt, 0)
                done(sp, act_tt, it, tt_qk(3, 3))
                passed()
                v_in.wait(sp, it, 8)
                store_kept(l, 1)
                if recur:
                    sp.wait_ge(lstm.gates_done, step(it, HALFS))
                    load_xw(0, step(it, SLOTS))
                pe_out.wait(sp, it, BATCH * KT)
                load_weight(1, nxt)
                pe_dd.wait(sp, it, dd_a(FCH - 1))
                load_weight(2, nxt)
                pe_out.wait(sp, it, BATCH * KT + KT)
                load_weight(3, nxt)
                if recur:
                    sp.wait_ge(lstm.gates_done, step(it, SLOTS))
                    load_xw(1, step(it, SLOTS + HALFS))

            sp.dma_start(mask[:, :, :], masks.rearrange("a p n -> p a n")).then_inc(cst_in, 16)
            sp.dma_start(rot[:, :, :].rearrange("p t (a d) -> p t a d", a=4), rotary.rearrange("(t p) a d -> p t a d", p=P)).then_inc(cst_in, 16)
            load_scales(0)
            sp.wait_ge(cleared, NCLEAR)
            load_kept(0, 0)
            load_xw(0, LEAD)
            load_xw(1, LEAD + HALFS)
            sp.sem_inc(kept_out, 32)

            def chunk(c, recur):
                sp.wait_ge(stored, c * 16 + 16)
                passed()
                sp.dma_start(xres[:, :, :].rearrange("p k (b t) -> p k b t", b=BATCH),
                             x_cols.rearrange("p k (b t) -> p k b t", b=BATCH)[:, :, :, bass.ds(c * CHUNK, CHUNK)]).then_inc(xres_in, 16)
                with sp.Fori(0, DEPTH - 1) as l:
                    body(c, l, l + c * DEPTH, recur, l + 1)
                body(c, DEPTH - 1, c * DEPTH + (DEPTH - 1), recur, 0)
                sp.wait_ge(xres_sum, (c + 1) * KT)
                passed()
                sp.dma_start(out.rearrange("p k (b t) -> p k b t", b=BATCH)[:, :, :, bass.ds(c * CHUNK, CHUNK)],
                             xres[:, :, :].rearrange("p k (b t) -> p k b t", b=BATCH)).then_inc(stored, 16)

            with sp.Fori(0, CHUNKS - 1) as c:
                chunk(c, True)
            chunk(CHUNKS - 1, False)
            sp.wait_ge(stored, (CHUNKS + 1) * 16)
            sp.wait_ge(kept_out, CHUNKS * DEPTH * 64 + 32)

        @block.gpsimd
        def _(pool):
            nc.gpsimd.memset(edge_a[:, :, :], 0.0).then_inc(cleared, 1)
            nc.gpsimd.memset(edge_b[:, :, :], 0.0).then_inc(cleared, 1)
            nc.gpsimd.memset(power[:, :], -0.5).then_inc(cleared, 1)
            nc.gpsimd.memset(kT[:, :, :, :], 0.0).then_inc(cleared, 1)
            nc.gpsimd.memset(va[:, :, :], 0.0).then_inc(cleared, 1)
            pool.wait_ge(cleared, NCLEAR)
            pool.wait_ge(cst_in, 32)

            def passed():
                pool.sem_inc(pool_passed, 1)

            def edge_to(buf, edge, l, count, it):
                passed()
                count.wait(pool, it, count.inc(nc.gpsimd.tensor_copy(buf[:, 1, :, 0:1].rearrange("p b t -> p (b t)"),
                                                                     edge[:, bass.ds(l, 1), :].rearrange("p a b -> p (a b)"))))

            def edge_from(buf, edge, l, count):
                passed()
                count.inc(nc.gpsimd.tensor_copy(edge[:, bass.ds(l, 1), :].rearrange("p a b -> p (a b)"),
                                                buf[:, 1, :, ROW - 1:ROW].rearrange("p b t -> p (b t)")))

            def turns(i, it):
                for c in range(4):
                    use = 4 * i + c + 1
                    done(pool, act_mm, it, mm_q(i, c))
                    qk_in.wait(pool, it, use + 2)
                    src = raw[:, c, :].rearrange("p (h a d) -> p h a d", a=2, d=HALF)
                    dst = turn[:, c % 2, :].rearrange("p (h a d) -> p h a d", a=2, d=HALF)
                    tab = rotl[:, i % TPC, 2 * (c % 2) + 1:2 * (c % 2) + 2, :].rearrange("p o (a d) -> p o a d", a=2)
                    for a in range(2):
                        ins = nc.gpsimd.tensor_tensor(dst[:, :, a, :], src[:, :, 1 - a, :],
                                                      tab[:, :, a, :].broadcast_to([P, 8, HALF]), ALU.mult)
                    turn_in.inc(ins)
                    ss_in.wait(pool, it, use)
                    hs = slice(8 * (c // 2), 8 * (c // 2) + 8)
                    norm_in.inc(nc.gpsimd.tensor_tensor(qn[:, i % 2, hs] if c % 2 == 0 else kn[:, hs], ss[:, c, :], power[:, 0:8], ALU.pow))

            def values_up(i, it):
                v_in.wait(pool, it, 2 * i + 2)
                if i == 0:
                    ffn_out.wait(pool, it, KT)
                else:
                    pe_dd.wait(pool, it, dd_o(i - 1, 1))
                norm_in.wait(pool, it, 4 if i == 0 else 4 * TPG)
                passed()
                vup_in.wait(pool, it, vup_in.inc(nc.gpsimd.tensor_copy(va[WINDOW:P, 1, :], vb[WINDOW:P, 0, :])))

            def body(c, l, it, recur):
                pool.wait_ge(sc_in, (it + 1) * 16)
                done(pool, qk_in, it, 0)
                passed()
                nc.gpsimd.tensor_tensor(rotl[:, :, :, :].rearrange("p t a d -> p t (a d)"), rot[:, bass.ds(c * TPC, TPC), :],
                                        scales[:, :].rearrange("p (o n) -> p o n", o=1).broadcast_to([P, TPC, 4 * DHEAD]),
                                        ALU.mult).then_inc(rotl_in, 1)
                pool.wait_ge(chunk_in, c + 1)
                ffn_out.wait(pool, it, 1)
                edge_to(xa, edge_a, l, edge_a_in, it)
                edge_from(xa, edge_a, l, edge_a_in)
                edge_to(xb, edge_b, l, edge_b_in, it)
                ffn_out.wait(pool, it, KT)
                nc.gpsimd.tensor_copy(vec[:, :], vecs[:, bass.ds(l, 1), :].rearrange("p a n -> p (a n)")).then_inc(vec_in, 1)
                pool.wait_ge(rotl_in, it + 1)
                turns(0, it)
                values_up(0, it)
                turns(1, it)
                turns(2, it)
                turns(3, it)
                values_up(2, it)
                for b in range(BATCH):
                    var_in.wait(pool, it, b + 1)
                    ts = slice(TPC * b, TPC * b + TPC)
                    rstd_in.inc(nc.gpsimd.tensor_tensor(rstd[:, ts], mv[:, ts, 1], power[:, 0:TPC], ALU.pow))
                attn_out.wait(pool, it, BATCH * KT)
                edge_from(xb, edge_b, l, edge_b_in)

            passes(pool, body)

        @block.tensor
        def _(pe):
            pe.wait_ge(cleared, NCLEAR)
            pe.wait_ge(cst_in, 32)

            def body(c, l, it, recur):
                slot = [0]

                def lstm_step():
                    if recur:
                        n = slot[0]
                        slot[0] += 1
                        if n % HALFS == 0:
                            pe.wait_ge(xw_in[n // HALFS], (it + 1) * 16)
                        lstm.on_pe(nc, pe, step(it, n), gates, gates, ident16, xwp[:, n, :])

                def project(i, chunks):
                    for c_ in chunks:
                        col = (c_ // 2) * 512 + (c_ % 2) * INNER if c_ < 4 else 2 * INNER + (c_ - 4) * 512
                        use = mm_q(i, c_)
                        freed(pe, act_mm, it, use)
                        for k in (1, 0):
                            if use == 1:
                                ffn_out.wait(pe, it, 2 - k)
                            last = nc.tensor.matmul(bank(mm, use)[:, :], columns(xa, i, k, True), wqkv[:, k, col:col + 512],
                                                    start=(k == 1), stop=(k == 0))
                        pe_mm.inc(last)

                def turn_qk(i, chunks):
                    for c_ in chunks:
                        use = tt_qk(i, c_)
                        done(pe, qk_in, it, 4 * i + c_ + 1)
                        freed(pe, act_tt, it, use)
                        for j in range(4):
                            last = nc.tensor.transpose(bank(tt, use)[:, j * TILE:(j + 1) * TILE], qk[:, c_, j * P:(j + 1) * P], ident[:, :])
                        pe_tt.inc(last)

                def scores(i, g):
                    use = HG * i + g + 1
                    freed(pe, act_st, it, use)
                    done(pe, act_tt, it, tt_qk(i, 1 if g < 2 else 3))
                    if i % TPC == 0 and g == 0:
                        pe.wait_ge(kept_in, it * 64 + (32 if i == 0 else 64))
                    which = c if i % TPC == 0 else 1
                    bk = bank(st, use)
                    nc.tensor.matmul(bk[:, :].rearrange("p (g n) -> p g n", g=HG), ident16[:, :],
                                     mask[:, bass.ds(which, 1), :].broadcast_to([P, HG, TILE]), start=True, stop=False, skip_group_check=True)
                    for w in range(2):
                        for n in range(HG):
                            pair, lo = 4 * (g // 2) + n, DHEAD * (g % 2)
                            keys = kT[lo:lo + DHEAD, i % 2, pair, :].rearrange("p (c x) -> p c x", x=WINDOW)
                            keys = keys[:, 0:3:2, :] if w == 0 else keys[:, 0:2, :]
                            last = nc.tensor.matmul(bk[w * WINDOW:(w + 1) * WINDOW, n * TILE:(n + 1) * TILE].rearrange("p (c x) -> p c x", x=WINDOW),
                                                    qT[lo:lo + DHEAD, pair, w * WINDOW:(w + 1) * WINDOW], keys,
                                                    start=False, stop=(n == HG - 1), skip_group_check=True)
                    pe_st.inc(last)

                def turn_p(i, g):
                    use = tt_p(i, g)
                    pr_in.wait(pe, it, HG * i + g + 1)
                    freed(pe, act_tt, it, use)
                    for n in range(HG):
                        last = nc.tensor.transpose(bank(tt, use)[:, n * TILE:(n + 1) * TILE], pr[:, g % 2, n * TILE:(n + 1) * TILE], ident[:, :])
                    pe_tt.inc(last)

                def values(i, g):
                    use = dd_o(i, g // 2)
                    if g % 2 == 0:
                        freed(pe, dve_dd, it, use)
                    v_in.wait(pe, it, 2 * i + g // 2 + 1)
                    if i % TPC == 1 and g == 0:
                        vup_in.wait(pe, it, i // TPC + 1)
                    done(pe, act_tt, it, tt_p(i, g))
                    bk = bank(dd, use)
                    for n in range(HG):
                        head = head_of(g, n)
                        lo, col = DHEAD * (g % 2), n * TILE
                        for w, v in ((0, va), (1, vb)):
                            last = nc.tensor.matmul(bk[lo:lo + DHEAD, col + w * WINDOW:col + (w + 1) * WINDOW],
                                                    v[:, i % 2, head * DHEAD:(head + 1) * DHEAD],
                                                    pT[:, g % 2, n * TILE + w * WINDOW:n * TILE + (w + 1) * WINDOW],
                                                    start=True, stop=True, skip_group_check=True)
                    if g % 2 == 1:
                        pe_dd.inc(last)

                pe.wait_ge(chunk_in, c + 1)
                edge_a_in.wait(pe, it, 1)
                pe.wait_ge(wqkv_in, (it + 1) * 16)
                def wo_first_heads(m):
                    if m == 0:
                        pe.wait_ge(wo_in, (it + 1) * 16)
                        done(pe, act_mm, it, 6 * TPG)
                        done(pe, dve_dd, it, dd_o(TPG - 1, 0))
                    for k in range(INNER // P // 2):
                        nc.tensor.matmul(mm[m][:, :], wo[:, k, m * P:(m + 1) * P], oT[:, k, :], start=(k == 0), stop=False, skip_group_check=True)

                def wo_last_heads(b, m):
                    done(pe, dve_dd, it, dd_o(TPC * b + TPC - 1, 1))
                    ts = slice(b * CHUNK, (b + 1) * CHUNK)
                    for k in range(INNER // P // 2, INNER // P):
                        last = nc.tensor.matmul(mm[m][:, ts], wo[:, k, m * P:(m + 1) * P], oT[:, k, ts], start=False,
                                                stop=(k == INNER // P - 1), skip_group_check=True)
                    pe_out.inc(last)

                def turn_stream(b):
                    done(pe, act_st, it, HG * TPG - 1 + b)
                    attn_out.wait(pe, it, KT * (b + 1))
                    edge_b_in.wait(pe, it, 1)
                    for i in range(TPC):
                        for k in range(KT):
                            last = nc.tensor.transpose(st[b][:, (i * KT + k) * P:(i * KT + k + 1) * P],
                                                       columns(xb, TPC * b + i, k, True), ident[:, :])
                    pe_ft.inc(last)

                def turn_back(b):
                    xn_in.wait(pe, it, b + 1)
                    for k in range(KT):
                        use = tt_ln(b, k)
                        freed(pe, act_tt, it, use)
                        for i in range(TPC):
                            last = nc.tensor.transpose(bank(tt, use)[:, i * TILE:(i + 1) * TILE], xn[:, TPC * b + i, k * P:(k + 1) * P], ident[:, :])
                        pe_tt.inc(last)

                project(0, (0, 1))
                lstm_step()
                project(0, (2, 3))
                lstm_step()
                project(0, (4, 5))
                lstm_step()
                project(1, (0,))
                turn_qk(0, (0, 1))
                for i in range(TPG):
                    more = i + 1 < TPG
                    if more:
                        lstm_step()
                    scores(i, 0)
                    if i > 0:
                        turn_p(i - 1, 3)
                    if more:
                        project(i + 1, (1,))
                    lstm_step()
                    if i > 0:
                        values(i - 1, 3)
                    turn_qk(i, (2, 3))
                    if more:
                        project(i + 1, (2,))
                    if not more:
                        lstm_step()
                    scores(i, 1)
                    turn_p(i, 0)
                    lstm_step()
                    scores(i, 2)
                    values(i, 0)
                    turn_p(i, 1)
                    if more:
                        project(i + 1, (3,))
                    lstm_step()
                    values(i, 1)
                    if more:
                        turn_qk(i + 1, (0, 1))
                        project(i + 1, (4,))
                    if more:
                        lstm_step()
                    scores(i, 3)
                    turn_p(i, 2)
                    if more:
                        project(i + 1, (5,))
                    else:
                        wo_first_heads(0)
                    lstm_step()
                    values(i, 2)
                    if i + 2 < TPG:
                        project(i + 2, (0,))
                wo_first_heads(1)
                turn_p(TPG - 1, 3)
                lstm_step()
                wo_last_heads(0, 0)
                lstm_step()
                wo_last_heads(0, 1)
                values(TPG - 1, 3)
                lstm_step()
                turn_stream(0)
                for m in range(KT):
                    wo_last_heads(1, m)
                lstm_step()
                turn_back(0)
                turn_stream(1)
                lstm_step()
                lstm_step()
                turn_back(1)
                pe.wait_ge(w1_in, (it + 1) * 16)
                for j in range(FCH):
                    for use, bk, src, cnt, col in ((mm_gate(j), mm, act_mm, pe_mm, FF), (dd_a(j), dd, dve_dd, pe_dd, 0)):
                        freed(pe, src, it, use)
                        for k in range(KT):
                            if j == 0 and cnt is pe_mm:
                                done(pe, act_tt, it, tt_ln(BATCH - 1, k))
                            last = nc.tensor.matmul(bank(bk, use)[0:FW[j], :], w1[:, k, col + j * P:col + j * P + FW[j]], xnT[:, k, :],
                                                    start=(k == 0), stop=(k == KT - 1))
                        cnt.inc(last)
                        if cnt is pe_mm and j in DENSE:
                            lstm_step()
                    lstm_step()
                pe.wait_ge(w2_in, (it + 1) * 16)
                for n, m in enumerate((1, 0)):
                    done(pe, act_mm, it, mm_gate(FCH - 2 + n))
                    for k in range(FCH):
                        if n == 0 and k == FCH - 1:
                            done(pe, dve_dd, it, dd_a(FCH - 1))
                        elif n == 0 and k == 0:
                            done(pe, dve_dd, it, dd_a(FCH - 2))
                        elif n == 1 and k == FCH // 2:
                            lstm_step()
                        last = nc.tensor.matmul(mm[n][:, :], w2[0:FW[k], k, m * P:(m + 1) * P], u[0:FW[k], k, :],
                                                start=(k == 0), stop=(k == FCH - 1), skip_group_check=True)
                    pe_out.inc(last)
                    if n == 0:
                        lstm_step()
                assert slot[0] in (0, SLOTS), slot[0]

            passes(pe, body)

        @block.scalar
        def _(act):
            act.sem_inc(act_mm.sem, act_mm.start)
            act.sem_inc(act_tt.sem, act_tt.start)
            act.sem_inc(act_st.sem, act_st.start)
            act.wait_ge(cleared, NCLEAR)

            def copy(dst, src, **kw):
                return nc.scalar.activation(dst, src, ACT.Identity, **kw)

            def body(c, l, it, recur):
                slot = [0]

                def lstm_step():
                    if recur:
                        lstm.on_act(nc, act, step(it, slot[0]), False)
                        slot[0] += 1

                def take_qk(i, c_):
                    use, n = mm_q(i, c_), 4 * i + c_ + 1
                    pe_mm.wait(act, it, use)
                    qk_in.wait(act, it, n)
                    src = bank(mm, use)
                    nc.scalar.activation(sq[:, c_, :], src[:, :], ACT.Square)
                    act_mm.inc(copy(raw[:, c_, :], src[:, :]))

                def take_v(i, c_):
                    use = mm_q(i, c_)
                    pe_mm.wait(act, it, use)
                    src = bank(mm, use)
                    cols = slice((c_ - 4) * 512, (c_ - 3) * 512)
                    v_in.inc(copy(vb[:, i % 2, cols], src[:, :]))
                    act_mm.inc(copy(va[0:WINDOW, i % 2, cols], src[0:WINDOW, :]))

                def take_turned(i, c_):
                    use = tt_qk(i, c_)
                    pe_tt.wait(act, it, use)
                    src = bank(tt, use)[:, :].rearrange("p (j t) -> p j t", j=4)
                    pairs_ = slice((c_ // 2) * 4, (c_ // 2) * 4 + 4)
                    if c_ % 2 == 0:
                        act_tt.inc(copy(qT[:, pairs_, :], src))
                    else:
                        if c_ == 1 and i % TPC == 1:
                            act.wait_ge(kept_out, it * 64 + 32 * (i // TPC) + 32)
                        if i % TPC == 0:
                            copy(kT[:, 1, pairs_, 2 * WINDOW:3 * WINDOW], src[:, :, WINDOW:2 * WINDOW])
                        act_tt.inc(copy(kT[:, i % 2, pairs_, 0:2 * WINDOW], src))

                def exps(i, g):
                    use = HG * i + g + 1
                    nb_in.wait(act, it, use)
                    src = bank(st, use)
                    for n in range(HG):
                        head, at = head_of(g, n), HG * g + n
                        ins = nc.scalar.activation(pr[:, g % 2, n * TILE:(n + 1) * TILE], src[:, n * TILE:(n + 1) * TILE], ACT.Exp,
                                                   bias=nb[:, at:at + 1], scale=qn[:, i % 2, head:head + 1],
                                                   accum_out=den[:, at:at + 1])
                    act_st.inc(ins)

                def take_p(i, g):
                    use = tt_p(i, g)
                    pe_tt.wait(act, it, use)
                    act_tt.inc(copy(pT[:, g % 2, :], bank(tt, use)[:, :]))

                take_qk(0, 0)
                take_qk(0, 1)
                lstm_step()
                take_qk(0, 2)
                take_qk(0, 3)
                lstm_step()
                take_v(0, 4)
                take_v(0, 5)
                lstm_step()
                take_qk(1, 0)
                take_turned(0, 0)
                take_turned(0, 1)
                for i in range(TPG):
                    more = i + 1 < TPG
                    if more:
                        lstm_step()
                    if i > 0:
                        take_p(i - 1, 3)
                    exps(i, 0)
                    if more:
                        take_qk(i + 1, 1)
                    lstm_step()
                    take_turned(i, 2)
                    take_turned(i, 3)
                    if more:
                        take_qk(i + 1, 2)
                    if not more:
                        lstm_step()
                    take_p(i, 0)
                    exps(i, 1)
                    lstm_step()
                    take_p(i, 1)
                    exps(i, 2)
                    if more:
                        take_qk(i + 1, 3)
                    lstm_step()
                    if more:
                        take_turned(i + 1, 0)
                        take_turned(i + 1, 1)
                        take_v(i + 1, 4)
                    if more:
                        lstm_step()
                    take_p(i, 2)
                    exps(i, 3)
                    if more:
                        take_v(i + 1, 5)
                    lstm_step()
                    if i + 2 < TPG:
                        take_qk(i + 2, 0)
                take_p(TPG - 1, 3)
                for _ in range(4):
                    lstm_step()
                act.wait_ge(vec_in, it + 1)

                def take_normalised(b):
                    for k in range(KT):
                        use = tt_ln(b, k)
                        pe_tt.wait(act, it, use)
                        act_tt.inc(copy(xnT[:, k, b * CHUNK:(b + 1) * CHUNK], bank(tt, use)[:, 0:CHUNK], bias=vcol(LNB + k), scale=vcol(LNG + k)))

                take_normalised(0)
                lstm_step()
                lstm_step()
                take_normalised(1)
                for j in range(FCH):
                    use = mm_gate(j)
                    pe_mm.wait(act, it, use)
                    if j >= 2:
                        done(act, dve_dd, it, dd_a(j - 2))
                    act_mm.inc(nc.scalar.activation(gel[0:FW[j], j % 2, :], bank(mm, use)[0:FW[j], :], ACT.Gelu,
                                                    bias=vec[0:FW[j], B1G + j:B1G + j + 1]))
                    lstm_step()
                    if j in DENSE:
                        lstm_step()
                lstm_step()
                lstm_step()
                assert slot[0] in (0, SLOTS), slot[0]

            passes(act, body)

        @block.vector
        def _(dve):
            dve.sem_inc(dve_dd.sem, dve_dd.start)
            dve.sem_inc(qk_in.sem, qk_in.start)
            dve.sem_inc(ffn_out.sem, ffn_out.start)
            dve.sem_inc(stored, 16)
            dve.wait_ge(cleared, NCLEAR)

            def chunk_start(c):
                dve.wait_ge(lstm.history, (c + 1) * CHUNK)
                for k in range(KT):
                    ins = nc.vector.tensor_copy(tokens(xa, k), lstm.hist[:, bass.ds(c * CHUNK, CHUNK), k * BATCH:(k + 1) * BATCH].rearrange("p t b -> p b t"))
                ins.then_inc(chunk_in, 1)

            def chunk_end(c):
                ffn_out.wait(dve, c * DEPTH + DEPTH, KT)
                dve.wait_ge(xres_in, (c + 1) * 16)
                for k in range(KT):
                    nc.vector.tensor_tensor(by_batch(xres[:, k, :]), tokens(xa, k), by_batch(xres[:, k, :]), ALU.add).then_inc(xres_sum, 1)
                dve.wait_ge(xres_sum, (c + 1) * KT)

            def body(c, l, it, recur):
                slot = [0]

                def lstm_step():
                    if recur:
                        lstm.on_dve(nc, dve, step(it, slot[0]), gates, gates)
                        slot[0] += 1

                def link(ins):
                    chain.wait(dve, it, chain.inc(ins))

                def rotate(i, c_):
                    done(dve, act_mm, it, mm_q(i, c_))
                    tab = rotl[:, i % TPC, 2 * (c_ % 2):2 * (c_ % 2) + 1, :]
                    nc.vector.tensor_tensor(heads(qk[:, c_, :]), heads(raw[:, c_, :]), tab.broadcast_to([P, 8, DHEAD]), ALU.mult)
                    link(nc.vector.tensor_reduce(ss[:, c_, :], heads(sq[:, c_, :]), AX_X, ALU.add))
                    ss_in.inc(nc.vector.tensor_scalar(ss[:, c_, :], ss[:, c_, :], NORM_FLOOR, None, ALU.max))

                def finish(i, c_):
                    n = 4 * i + c_ + 1
                    dst = heads(qk[:, c_, :])
                    hs = slice(8 * (c_ // 2), 8 * (c_ // 2) + 8)
                    turn_in.wait(dve, it, n)
                    ins = nc.vector.tensor_tensor(qk[:, c_, :], qk[:, c_, :], turn[:, c_ % 2, :], ALU.add)
                    if c_ % 2 == 1:
                        link(ins)
                        norm_in.wait(dve, it, n)
                        ins = nc.vector.tensor_tensor(dst, dst, kn[:, hs].rearrange("p (h o) -> p h o", o=1).broadcast_to([P, 8, DHEAD]), ALU.mult)
                    qk_in.inc(ins)

                def maxima(i, g):
                    use = HG * i + g + 1
                    hs = slice(HG * g, HG * g + HG)
                    pe_st.wait(dve, it, use)
                    norm_in.wait(dve, it, 4 * i + 2 * (g // 2) + 1)
                    link(nc.vector.tensor_reduce(mx[:, hs], heads(bank(st, use)[:, :], HG), AX_X, ALU.max))
                    nb_in.inc(nc.vector.scalar_tensor_tensor(nb[:, hs], mx[:, hs], -1.0, qn[:, i % 2, head_of(g, 0):head_of(g, HG - 1) + 1:2], ALU.mult, ALU.mult))

                def normalise(i, g):
                    use = HG * i + g + 1
                    hs = slice(HG * g, HG * g + HG)
                    done(dve, act_st, it, use)
                    link(nc.vector.reciprocal(rden[:, hs], den[:, hs]))
                    dst = heads(pr[:, g % 2, :], HG)
                    pr_in.inc(nc.vector.tensor_tensor(dst, dst, rden[:, hs].rearrange("p (h o) -> p h o", o=1).broadcast_to([P, HG, TILE]), ALU.mult))

                def take_o(i, half):
                    use = dd_o(i, half)
                    pe_dd.wait(dve, it, use)
                    dve_dd.inc(nc.vector.tensor_copy(oT[:, 4 * half:4 * half + 4, i * TILE:(i + 1) * TILE],
                                                     bank(dd, use)[:, :].rearrange("p (j t) -> p j t", j=4)))

                def add_attention(b, m):
                    pe_out.wait(dve, it, KT * b + m + 1)
                    attn_out.inc(nc.vector.tensor_tensor(xb[:, m, b, m:m + CHUNK], mm[m][:, b * CHUNK:(b + 1) * CHUNK], xa[:, m, b, m:m + CHUNK], ALU.add))

                def statistics(b):
                    pe_ft.wait(dve, it, b + 1)
                    for i in range(TPC):
                        n = chain.inc(nc.vector.bn_stats(stats[:, TPC * b + i, :], st[b][:, i * DIM:(i + 1) * DIM]))
                    chain.wait(dve, it, n)
                    dve.sem_inc(dve_passed, 1)
                    for i in range(TPC * b, TPC * b + TPC):
                        n = chain.inc(nc.vector.bn_aggr(mv[:, i, :], stats[:, i, :]))
                    chain.wait(dve, it, n)
                    ts = slice(TPC * b, TPC * b + TPC)
                    var_in.inc(nc.vector.tensor_scalar(mv[:, ts, 1], mv[:, ts, 1], LN_EPS, None, ALU.add))

                def standardise(b):
                    rstd_in.wait(dve, it, b + 1)
                    for i in range(TPC):
                        t = TPC * b + i
                        ins = nc.vector.tensor_scalar(xn[:, t, :], st[b][:, i * DIM:(i + 1) * DIM], mv[:, t, 0:1], rstd[:, t:t + 1], ALU.subtract, ALU.mult)
                    xn_in.inc(ins)

                dve.wait_ge(rotl_in, it + 1)
                rotate(0, 0)
                lstm_step()
                rotate(0, 1)
                lstm_step()
                rotate(0, 2)
                finish(0, 0)
                finish(0, 1)
                lstm_step()
                rotate(0, 3)
                finish(0, 2)
                for i in range(TPG):
                    more = i + 1 < TPG
                    if more:
                        lstm_step()
                    maxima(i, 0)
                    if i == 0:
                        finish(0, 3)
                    if more:
                        rotate(i + 1, 0)
                    lstm_step()
                    normalise(i, 0)
                    if i > 0:
                        take_o(i - 1, 1)
                    if more:
                        rotate(i + 1, 1)
                    if not more:
                        lstm_step()
                    maxima(i, 1)
                    if more:
                        finish(i + 1, 0)
                    lstm_step()
                    normalise(i, 1)
                    maxima(i, 2)
                    if more:
                        finish(i + 1, 1)
                        rotate(i + 1, 2)
                    lstm_step()
                    normalise(i, 2)
                    take_o(i, 0)
                    if more:
                        rotate(i + 1, 3)
                    if more:
                        lstm_step()
                    maxima(i, 3)
                    if more:
                        finish(i + 1, 2)
                    lstm_step()
                    normalise(i, 3)
                    if more:
                        finish(i + 1, 3)
                lstm_step()
                add_attention(0, 0)
                lstm_step()
                add_attention(0, 1)
                take_o(TPG - 1, 1)
                lstm_step()
                statistics(0)
                standardise(0)
                for m in range(KT):
                    add_attention(1, m)
                lstm_step()
                statistics(1)
                lstm_step()
                standardise(1)
                lstm_step()
                dve.wait_ge(vec_in, it + 1)
                attn_out.wait(dve, it, BATCH * KT)
                for j in range(FCH):
                    if j in DENSE:
                        lstm_step()
                    use = dd_a(j)
                    pe_dd.wait(dve, it, use)
                    done(dve, act_mm, it, mm_gate(j))
                    w = FW[j]
                    dve_dd.inc(nc.vector.scalar_tensor_tensor(u[0:w, j, :], bank(dd, use)[0:w, :], vec[0:w, B1A + j:B1A + j + 1], gel[0:w, j % 2, :],
                                                              ALU.add, ALU.mult))
                    lstm_step()
                for n, m in enumerate((1, 0)):
                    pe_out.wait(dve, it, BATCH * KT + n + 1)
                    ffn_out.inc(nc.vector.scalar_tensor_tensor(tokens(xa, m), by_batch(mm[n][:, :]), vcol(B2 + m), tokens(xb, m), ALU.add, ALU.add))
                    if n == 0:
                        lstm_step()
                        lstm_step()
                assert slot[0] in (0, SLOTS), slot[0]

            passes(dve, body, chunk_start, chunk_end)
            for n in COUNTS:
                n.check(2)


def rotary_tables(np):
    half = np.arange(0, DHEAD, 2, dtype=np.float32)
    inv_freq = (1.0 / np.float32(10000.0) ** (half / np.float32(DHEAD))).astype(np.float32)
    t = np.arange(SEQ, dtype=np.float32)
    freqs = t[:, None] * inv_freq[None, :]
    freqs = np.concatenate([freqs, freqs], -1)
    base = (half + np.float32(0.4 * DHEAD)) / np.float32(1.4 * DHEAD)
    power = (t - SEQ // 2) / np.float32(WINDOW // 2)
    scale = (base[None, :] ** power[:, None]).astype(np.float32)
    scale = np.concatenate([scale, scale], -1)
    sign = np.concatenate([-np.ones(DHEAD // 2), np.ones(DHEAD // 2)]).astype(np.float32)
    cos, sin = np.cos(freqs), np.sin(freqs) * sign
    return np.stack([QK_SCALE * cos * scale, QK_SCALE * sin * scale, cos / scale, sin / scale], 1).astype(np.float32)


def window_masks(np):
    i, j = np.arange(WINDOW)[:, None], np.arange(WINDOW)[None, :]
    own, before = np.where(j <= i, 0.0, MASKED), np.where(j >= i, 0.0, MASKED)
    none = np.full((WINDOW, WINDOW), MASKED)
    second = np.concatenate([before, own], 1)
    return np.stack([np.concatenate([np.concatenate([own, b], 1), second], 0) for b in (none,) + (before,) * (CHUNKS - 1)])


def kernel(x, cond_1024, L0_cond_Wx, L0_cond_Wh, L0_cond_b, L0_ffn_Wqkv, L0_ffn_q_scale, L0_ffn_k_scale, L0_ffn_Wo,
           L0_ffn_ln_g, L0_ffn_ln_b, L0_ffn_W1, L0_ffn_b1, L0_ffn_W2, L0_ffn_b2):
    import ml_dtypes
    import numpy as np
    import concourse.bacc as bacc
    from concourse.bass_utils import run_bass_kernel_spmd

    def rows(w):
        w = np.asarray(w)
        pad = -w.shape[-2] % P
        w = np.concatenate([w, np.zeros((*w.shape[:-2], pad, w.shape[-1]), w.dtype)], -2)
        return np.swapaxes(w.reshape(*w.shape[:-2], -1, P, w.shape[-1]), -3, -2)

    def flat(w):
        return w.reshape(*w.shape[:-2], -1)

    def cols(v):
        return rows(np.asarray(v)[..., None])[..., 0]

    def gates(w):
        i, f, o, g = np.split(np.asarray(w), 4, -1)
        return np.concatenate([o, i, f, g], -1)

    b1 = np.asarray(L0_ffn_b1)
    vecs = np.concatenate([cols(v) for v in (b1[:, :FF], b1[:, FF:], L0_ffn_ln_g, L0_ffn_ln_b, L0_ffn_b2)], -1)
    q_scale, k_scale = np.asarray(L0_ffn_q_scale), np.asarray(L0_ffn_k_scale)
    swap = lambda v: np.roll(v, DHEAD // 2, -1)
    xh = np.asarray(x)
    nc = bacc.Bacc("TRN2", target_bir_lowering=False, num_devices=1)
    given = {
        "x_cols": rows(xh.transpose(2, 0, 1).reshape(DIM, BATCH * SEQ)),
        "h0_cols": flat(rows(np.asarray(cond_1024).T)),
        "Wx": rows(gates(L0_cond_Wx)), "Wh": rows(gates(L0_cond_Wh)), "b_cols": cols(gates(L0_cond_b)),
        "Wqkv": flat(rows(L0_ffn_Wqkv)), "qk_scales": np.concatenate([q_scale, swap(q_scale), k_scale, swap(k_scale)], -1),
        "Wo": flat(rows(L0_ffn_Wo)), "W1": flat(rows(L0_ffn_W1)), "W2": flat(rows(L0_ffn_W2)),
        "layer_vecs": np.swapaxes(vecs, 0, 1),
        "rotary": rotary_tables(np), "masks": window_masks(np).astype(ml_dtypes.bfloat16), "identity": np.eye(P, dtype=np.float32),
    }
    arrays = {f"in_{n}": np.ascontiguousarray(a) for n, a in given.items()}
    args = [nc.dram_tensor(n, a.shape, mybir.dt.from_np(a.dtype), kind="ExternalInput").ap() for n, a in arrays.items()]
    args.append(nc.dram_tensor("out_cols", (P, KT, BATCH * SEQ), F32, kind="ExternalOutput").ap())
    build_program(nc, *args)
    r = run_bass_kernel_spmd(nc, [arrays], core_ids=[0])
    got = np.asarray(r.results[0]["out_cols"])
    return np.ascontiguousarray(got.transpose(1, 0, 2).reshape(DIM, BATCH, SEQ).transpose(1, 2, 0))
```
